# Optimizing a Trainium2 kernel written in Bass

```python
import numpy as np
import jax
import jax.numpy as jnp

def _softmax(x, axis=-1):
    return jax.nn.softmax(x, axis=axis)

def _gelu(x):
    return jax.nn.gelu(x, approximate=True)

def _silu(x):
    return jax.nn.silu(x)

def _sigmoid(x):
    return jax.nn.sigmoid(x)

def _layernorm(x, axis=-1, eps=1e-05):
    m = jnp.mean(x, axis=axis, keepdims=True)
    v = jnp.var(x, axis=axis, keepdims=True)
    return (x - m) / jnp.sqrt(v + eps)

def _scatter_add(tgt, idx, src, axis=0):
    return tgt.at[idx].add(src)

def _segment_sum(src, seg, n):
    return jax.ops.segment_sum(src, seg, n)
kernel_name = 'mk_adaln_d1_jaxref_r8_70c74a'

def setup_inputs(seed: int=0):
    np.random.seed(seed)
    _w = jnp.asarray

    def _L0_attn_setup():
        import math
        import jax, jax.numpy as jnp
        import numpy as np
        HEADS = 16
        key = jax.random.key(seed)
        k1, k2, k3, k4, k5 = jax.random.split(key, 5)
        B, S, D = (2, 256, 128)
        return {'x': jax.random.normal(k1, (B, S, D), dtype=jnp.float32), 'Wqkv': jax.random.normal(k2, (3 * D, D), dtype=jnp.float32) * (1.0 / math.sqrt(D)), 'bqkv': jax.random.normal(k3, (3 * D,), dtype=jnp.float32) * 0.02, 'Wo': jax.random.normal(k4, (D, D), dtype=jnp.float32) * (1.0 / math.sqrt(D)), 'bo': jax.random.normal(k5, (D,), dtype=jnp.float32) * 0.02}
    _L0_attn_in = _L0_attn_setup()

    def _L0_ffn_setup():
        import jax, jax.numpy as jnp
        import numpy as np
        K_TOP = 2
        key = jax.random.key(seed)
        k1, k2, k3 = jax.random.split(key, 3)
        B, S, H, E = (4, 256, 128, 8)
        hidden_states = jax.random.normal(k1, (B, S, H), dtype=jnp.float32)
        router_w = jax.random.normal(k2, (E, H), dtype=jnp.float32) * 0.02
        expert_weights = jax.random.normal(k3, (E, H, H), dtype=jnp.float32) * 0.02
        return {'hidden_states': hidden_states, 'router_w': router_w, 'expert_weights': expert_weights}
    _L0_ffn_in = _L0_ffn_setup()
    _L0_c = _w((lambda *s: np.random.randn(*s).astype(np.float32) * 0.05)(4, 128))
    _L0_wmod = _w((lambda *s: np.random.randn(*s).astype(np.float32) * 0.05)(128, 6 * 128) * 128 ** (-0.5))
    _d = {'L0_attn_x': _L0_attn_in['x'], 'L0_attn_Wqkv': _L0_attn_in['Wqkv'], 'L0_attn_bqkv': _L0_attn_in['bqkv'], 'L0_attn_Wo': _L0_attn_in['Wo'], 'L0_attn_bo': _L0_attn_in['bo'], 'L0_ffn_router_w': _L0_ffn_in['router_w'], 'L0_ffn_expert_weights': _L0_ffn_in['expert_weights'], 'L0_c': _L0_c, 'L0_wmod': _L0_wmod}
    _x0 = _d['L0_attn_x']
    _d['L0_attn_x'] = jax.random.normal(jax.random.fold_in(jax.random.key(seed), 1), (4, 1024, 128), dtype=_x0.dtype)
    del _x0
    return _d

def reference(L0_attn_x, L0_attn_Wqkv, L0_attn_bqkv, L0_attn_Wo, L0_attn_bo, L0_ffn_router_w, L0_ffn_expert_weights, L0_c, L0_wmod):

    def _L0_attn_ref(x, Wqkv, bqkv, Wo, bo):
        import math
        import jax, jax.numpy as jnp
        import numpy as np
        HEADS = 16
        B, S, D = x.shape
        H = HEADS
        hd = D // H
        qkv = x @ Wqkv.T + bqkv
        qkv = qkv.reshape(B, H, S, 3 * hd)
        q, k, v = jnp.split(qkv, 3, axis=-1)
        scores = jnp.einsum('bhsd,bhtd->bhst', q, k) * (1.0 / math.sqrt(hd))
        attn = jax.nn.softmax(scores, axis=-1)
        vals = jnp.einsum('bhst,bhtd->bhsd', attn, v)
        vals = vals.reshape(B, S, D)
        return vals @ Wo.T + bo

    def _L0_ffn_ref(hidden_states, router_w, expert_weights):
        import jax, jax.numpy as jnp
        import numpy as np
        K_TOP = 2
        B, S, H = hidden_states.shape
        x = hidden_states.reshape(-1, H)
        logits = x @ router_w.T
        probs = jax.nn.softmax(logits, axis=-1)
        topk_vals, topk_idx = jax.lax.top_k(probs, K_TOP)
        topk_w = topk_vals / (topk_vals.sum(-1, keepdims=True) + 1e-06)
        expert_out = jnp.einsum('nh,eho->eno', x, expert_weights)
        combined = jnp.take_along_axis(expert_out.transpose(1, 0, 2), topk_idx[:, :, None], axis=1)
        combined = combined.transpose(1, 0, 2)
        remap_bias = jnp.take_along_axis(probs, topk_idx, axis=1).T[:, :, None]
        weights = topk_w.T[:, :, None]
        out = ((combined + remap_bias) * weights).sum(axis=0)
        return out.reshape(B, S, H)
    x = L0_attn_x
    mod = (_silu(L0_c) @ L0_wmod).reshape(L0_c.shape[0], 6, 1, -1)
    sa, ca, ga, sb, cb, gb = (mod[:, 0], mod[:, 1], mod[:, 2], mod[:, 3], mod[:, 4], mod[:, 5])
    ga = (2 * (ga >= 0) - 1) * jnp.maximum(jnp.abs(ga), 0.25)
    gb = (2 * (gb >= 0) - 1) * jnp.maximum(jnp.abs(gb), 0.25)
    h = _layernorm(x, axis=-1) * (1 + ca) + sa
    x = x + ga * _L0_attn_ref(h, L0_attn_Wqkv, L0_attn_bqkv, L0_attn_Wo, L0_attn_bo)
    h = _layernorm(x, axis=-1) * (1 + cb) + sb
    x = x + gb * _L0_ffn_ref(h, L0_ffn_router_w, L0_ffn_expert_weights)
    return x

_drawn_inputs = setup_inputs


def setup_inputs(seed=0):
    import zlib

    import numpy as np

    out = dict(_drawn_inputs(seed))
    spreads = {}
    factors = {'L0_attn_bqkv': 26.499, 'L0_attn_bo': 8.0}
    for name, (base, spread) in spreads.items():
        noise = np.random.default_rng([zlib.crc32(name.encode()), seed]).standard_normal(out[name].shape)
        drawn = base * np.exp(spread * noise) if base else spread * noise
        out[name] = jnp.asarray(drawn.astype(out[name].dtype))
    for name, factor in factors.items():
        out[name] = (out[name] * factor).astype(out[name].dtype)
    return out
```

```python
from contextlib import ExitStack

import concourse.bass as bass
from concourse import mybir

ALU = mybir.AluOpType
ACT = mybir.ActivationFunctionType
AX = mybir.AxisListType
F32 = mybir.dt.float32
BF16 = mybir.dt.bfloat16
U32 = mybir.dt.uint32
I32 = mybir.dt.int32

P = 128
HEADS = 16
PARTS = 3
EPS = 1e-5
TOP_EPS = 1e-6
GATE_MIN = 0.25
MAX_EXP = 30.0
SPAN_MAX = 90.0
FAR = -1e30
MAX_ROW = 96

SETUP_CT, SETUP_SILU, SETUP_MOD, SETUP_GATES, SETUP_ALL = 2, 8, 9, 13, 14


def reached(eng, sem, count):
    if not isinstance(count, int) or count > 0:
        eng.wait_ge(sem, count)


def reached_apart(eng, sem, count, past, past_count):
    if not isinstance(count, int):
        count = eng.to_reg(count)
        eng.wait_ge(past, past_count)
    reached(eng, sem, count)


def spread(ap, axis, n):
    ap = ap.unsqueeze(axis)
    shape = list(ap.shape)
    shape[axis] = n
    return ap.broadcast_to(shape)


def adaln_block(nc, x, Wqkv, bqkv, Wo, bo, router_w, expert_w, c, wmod, out):
    B, S, D = x.shape
    hd = D // HEADS
    J = HEADS
    R = S // HEADS
    G = P // R
    T = B * S // P
    TB = S // P
    NE = router_w.shape[0]
    TOK = R * J
    KT = TOK // P
    HALF = TOK // 2
    SLOTS = PARTS * PARTS * hd
    SCALE = float(hd) ** -0.5
    assert D == P and hd == 8 and G == 2 and HALF == 512 and T % 2 == 0

    x_tiles = x.rearrange("b s d -> (b s) d").rearrange("(t p) d -> p t d", p=P)
    out_tiles = out.rearrange("b s d -> (b s) d").rearrange("(t p) d -> t p d", p=P)

    with ExitStack() as ctx:
        def sb(name, shape, dt=F32):
            return ctx.enter_context(nc.sbuf_tensor(name, shape, dt))

        def sem(name):
            return ctx.enter_context(nc.semaphore(name))

        x_all = sb("x_all", [P, T, D])
        out_all = sb("out_all", [P, T, D])
        ident = sb("ident", [P, P])
        ident_b = sb("ident_b", [P, P], BF16)
        wqkv_in = sb("wqkv_in", [P, 3, D])
        wo_in = sb("wo_in", [P, D])
        router_in = sb("router_in", [NE, D])
        c_in = sb("c_in", [B, D])
        wmod_in = sb("wmod_in", [P, 6 * D])
        experts_in = sb("experts_in", [P, NE, D])
        bqkv_rows = sb("bqkv_rows", [P, 3 * D])
        bo_rows = sb("bo_rows", [P, D])
        wqkvT = sb("wqkvT", [P, 3 * D])
        woT = sb("woT", [P, D])
        routerT = sb("routerT", [P, NE])
        cT = sb("cT", [P, B])
        c_exp = sb("c_exp", [P, B])
        c_exp1 = sb("c_exp1", [P, B])
        c_sig = sb("c_sig", [P, B])
        siluT = sb("siluT", [P, B])
        silu_wide = sb("silu_wide", [P, B, P])
        mod_tab = sb("mod_tab", [P, T, 4])
        gate_flag = sb("gate_flag", [P, 2, B, D])
        gate_sign = sb("gate_sign", [P, 2, B, D])
        gate_size = sb("gate_size", [P, 2, B, D])
        gates = sb("gates", [P, 2, B, D])
        wo_gated = sb("wo_gated", [P, B, D])
        bo_gated = sb("bo_gated", [P, B, D])
        experts_gated = sb("experts_gated", [P, B, NE, D])
        bv = sb("bv", [P, KT, hd])
        expert_ids = sb("expert_ids", [P, NE])
        minus_half = sb("minus_half", [P, 1])

        stats1 = sb("stats1", [P, 6])
        moments1 = sb("moments1", [P, 2])
        var_eps1 = sb("var_eps1", [P, 1])
        rstd1 = sb("rstd1", [P, 1])
        xhat = sb("xhat", [P, D])
        hT = sb("hT", [P, P])
        qk = sb("qk", [P, 2, J, hd])
        qk_rest = sb("qk_rest", [P, 2, J, hd])
        parts = sb("parts", [P, 2, J, PARTS, hd], BF16)
        slots = sb("slots", [P, 2, J, P], BF16)
        squares = sb("squares", [P, 2, J, hd])
        norms = sb("norms", [P, J * 2])
        key_min = sb("key_min", [P, 1])
        head_far = sb("head_far", [P, G])
        norm_max = sb("norm_max", [P, 2 + G])
        norm_all = sb("norm_all", [P, 2 + G])
        products = sb("products", [P, 2])
        bounds_sq = sb("bounds_sq", [P, 2])
        bounds_cut = sb("bounds_cut", [P, 2])
        bounds = sb("bounds", [P, 2])
        signed_scale = sb("signed_scale", [P, 2])
        half = sb("half", [P, 2])
        span = sb("span", [P, 1])
        sigma = sb("sigma", [P, 1])
        minus_one_if = sb("minus_one_if", [P, 1])
        bounded_int = sb("bounded_int", [P, 2, 1], I32)
        shift = sb("shift", [P, 2, 1])
        key_stack = sb("key_stack", [P, 2, G, J, R], BF16)
        query_stack = sb("query_stack", [P, 2, G, J, R], BF16)
        values = sb("values", [P, 2, G, KT, 32])
        row_max = sb("row_max", [P, G * KT])
        max_rest = sb("max_rest", [P, G * KT])
        max_rest2 = sb("max_rest2", [P, G * KT])
        max_parts = sb("max_parts", [P, G * KT, PARTS], BF16)

        probs = sb("probs", [P, 2, G, TOK])
        attn = sb("attn", [P, 8, R])
        sums_inv = sb("sums_inv", [R, 8, 4])
        vals = sb("vals", [R, G, D])
        valsT = sb("valsT", [P, P])
        x_gated = sb("x_gated", [P, D])
        x1 = sb("x1", [P, D])
        stats2 = sb("stats2", [P, 6])
        moments2 = sb("moments2", [P, 2])
        var_eps2 = sb("var_eps2", [P, 1])
        rstd2 = sb("rstd2", [P, 1])
        x1hat = sb("x1hat", [P, D])
        h2T = sb("h2T", [P, P])
        top_logits = sb("top_logits", [P, 8])
        logits0 = sb("logits0", [P, NE])
        router_exp = sb("router_exp", [P, NE])
        router_sum = sb("router_sum", [P, 1])
        router_inv = sb("router_inv", [P, 1])
        router_p = sb("router_p", [P, NE])
        top_p = sb("top_p", [P, 8])
        top_id = sb("top_id", [P, 8], U32)
        top_idf = sb("top_idf", [P, 8])
        pair_sum = sb("pair_sum", [P, 1])
        pair_eps = sb("pair_eps", [P, 1])
        pair_inv = sb("pair_inv", [P, 1])
        pair_w = sb("pair_w", [P, 2])
        pair_pw = sb("pair_pw", [P, 2])
        bias_w = sb("bias_w", [P, 1])
        coef0 = sb("coef0", [P, NE])
        coef1 = sb("coef1", [P, NE])
        coef = sb("coef", [P, NE])
        weighted = sb("weighted", [P, NE, D])
        mixed = sb("mixed", [P, D])
        base = sb("base", [P, D])

        ps_scores = ctx.enter_context(nc.psum_tensor("ps_scores", [P, G, TOK], F32))
        ps_attn = ctx.enter_context(nc.psum_tensor("ps_attn", [P, 512], F32))
        ps_a = ctx.enter_context(nc.psum_tensor("ps_a", [P, 512], F32))
        ps_c = ctx.enter_context(nc.psum_tensor("ps_c", [P, 2, 512], F32))
        ps_a_b = ps_a[:].bitcast(BF16).rearrange("p (j r) -> p j r", r=P)

        x_first, x_rest, w_loaded, small_loaded, experts_loaded = (
            sem("x_first"), sem("x_rest"), sem("w_loaded"), sem("small_loaded"), sem("experts_loaded"))
        out_stored = sem("out_stored")
        ident0, ident_ready, pool_consts, stacks_zero, stacks_const = (
            sem("ident0"), sem("ident_ready"), sem("pool_consts"), sem("stacks_zero"), sem("stacks_const"))
        setup_dve, setup_pe, setup_act = sem("setup_dve"), sem("setup_pe"), sem("setup_act")
        experts_are_gated = sem("experts_are_gated")
        names = """
            stats1_done moments1_done var1_done rstd1_done xhat_done xhatT_done hT_done qk_ps_done v_ps_done
            qk_done values_done hi_done rest1_done mid_done rest2_done parts_done
            squares_done norms_done key_min_done norm_max_done norm_all_done
            key_min_sum_done products_done bounds_sq_done bounds_cut_done bounds_done span_done sigma_done bounded_done
            shift_done k_slots_done q_slots_done
            attn_saved sums_inv0 sums_inv1 vals_done valsT_ps_done valsT_done attn_proj_done x_gated_done x1_done
            stats2_done moments2_done var2_done rstd2_done x1hat_done x1hatT_done h2T_done logits_done
            top_logits_done logits0_done router_exp_done router_inv_done router_p_done top_p_done top_id_done
            top_idf_done pair_sum_done pair_eps_done pair_inv_done pair_w_done pair_pw_done bias_w_done
            coef0_done coef1_done coef_done
            base_done weighted_done mixed_done out_done
        """.split()
        ev = {n: sem(n) for n in names}
        scores_ready = [[sem(f"scores_ready_{k}_{g}") for g in range(G)] for k in range(KT)]
        probs_ready = [[sem(f"probs_ready_{k}_{g}") for g in range(G)] for k in range(KT)]
        pv_done = [sem(f"pv_done_{k}") for k in range(KT)]
        chunkT_done = [sem(f"chunkT_done_{k}") for k in range(4)]
        chunk_saved = [sem(f"chunk_saved_{k}") for k in range(4)]
        attnT_done = [sem(f"attnT_done_{k}") for k in range(2)]
        experts_done = [sem(f"experts_done_{k}") for k in range(2)]
        M_PE, M_DVE = G * KT + G, G * KT + 3 + G
        m_scores, m_taken = sem("m_scores"), sem("m_taken")

        def shape_chunk(c, parity):
            stack = key_stack if c < 2 else query_stack
            j0 = 8 * (c % 2)
            return stack[:, parity, :, j0:j0 + 8, :].rearrange("p g j r -> p j g r")

        def tiles(eng, tile, last):
            tile(0, 0, before=0, after=2)
            tile(1, 1, before=1, after=2)
            with eng.Fori(2, T - 2, 2) as i:
                even = nc.s_assert_within(i, 2, T - 4, skip_runtime_bounds_check_because="i goes up by twos from 2")
                tile(even, 0, before=2, after=2)
                tile(even + 1, 1, before=2, after=2)
            tile(T - 2, 0, before=2, after=1)
            tile(T - 1, 1, before=2, after=0)
            last()

        def plus(eng, t, n):
            return t + n if isinstance(t, int) else eng.snap(t + n)

        def batch_of(eng, t):
            return t // TB if isinstance(t, int) else eng.snap(t // TB, min_val=0, max_val=B - 1)

        block = ctx.enter_context(nc.Block())

        @block.sync
        def _(sp):
            sp.dma_start(x_all[:, 0:1, :], x_tiles[:, 0:1, :]).then_inc(x_first, 16)
            sp.dma_start(wqkv_in[:], Wqkv.rearrange("(k p) i -> p k i", p=P)).then_inc(w_loaded, 16)
            sp.dma_start(c_in[:], c).then_inc(small_loaded, 16)
            sp.dma_start(wmod_in[:], wmod).then_inc(small_loaded, 16)
            sp.dma_start(wo_in[:], Wo).then_inc(small_loaded, 16)
            sp.dma_start(router_in[:], router_w).then_inc(small_loaded, 16)
            sp.dma_start(bqkv_rows[:], bqkv.partition_broadcast(P)).then_inc(small_loaded, 16)
            sp.dma_start(bo_rows[:], bo.partition_broadcast(P)).then_inc(small_loaded, 16)
            sp.dma_start(x_all[:, 1:T, :], x_tiles[:, 1:T, :]).then_inc(x_rest, 16)
            sp.dma_start(experts_in[:], expert_w.rearrange("e h o -> h e o")).then_inc(experts_loaded, 16)

            def store(w):
                reached(sp, ev["out_done"], plus(sp, w, 1))
                src = out_all[:, w, :] if isinstance(w, int) else out_all[:, bass.ds(w, 1), :]
                dst = out_tiles[w] if isinstance(w, int) else out_tiles[bass.ds(w, 1)]
                if isinstance(w, int):
                    sp.dma_start(dst, src).then_inc(out_stored, 16)
                else:
                    sp.dma_start(dst.rearrange("t p d -> p t d"), src).then_inc(out_stored, 16)

            def tile(t, parity, before, after):
                if before == 2:
                    store(plus(sp, t, -2))

            def last():
                store(T - 2)
                store(T - 1)
            tiles(sp, tile, last)
            sp.wait_ge(out_stored, 16 * T)

        @block.gpsimd
        def _(pool):
            nc.gpsimd.memset(ident[:], 0.0).then_inc(ident0, 1)
            pool.wait_ge(ident0, 1)
            nc.gpsimd.affine_select(out=ident[:], in_=ident[:], compare_op=ALU.not_equal, fill=1.0, base=0,
                                    pattern=[[-1, P]], channel_multiplier=1).then_inc(ident_ready, 1)
            pool.wait_ge(ident_ready, 1)
            nc.gpsimd.tensor_copy(ident_b[:], ident[:]).then_inc(ident_ready, 1)
            for e in range(NE):
                nc.gpsimd.memset(expert_ids[:, e:e + 1], float(e))
            for g in range(G):
                nc.gpsimd.memset(head_far[:, g:g + 1], FAR)
            for n in range(2):
                nc.gpsimd.memset(signed_scale[:, n:n + 1], (1 - 2 * n) * SCALE * SCALE)
            nc.gpsimd.memset(half[:], 0.5)
            nc.gpsimd.memset(minus_half[:], -0.5).then_inc(pool_consts, 1)
            pool.wait_ge(pool_consts, 1)
            for g in range(G):
                nc.gpsimd.memset(head_far[g * R:(g + 1) * R, g:g + 1], 0.0).then_inc(pool_consts, 1)
                pool.wait_ge(pool_consts, 2 + g)

            def rstd(u1, stats, var_eps, out_, done_in, done_var, done_out):
                reached_apart(pool, ev[done_in], u1, x_rest, 16)
                nc.gpsimd.tensor_scalar(var_eps[:], stats[:, 1:2], EPS, 1.0, ALU.add, ALU.mult).then_inc(ev[done_var], 1)
                reached(pool, ev[done_var], u1)
                nc.gpsimd.tensor_tensor(out_[:], var_eps[:], minus_half[:], ALU.pow).then_inc(ev[done_out], 1)

            def norms_of_tile(u1, parity, probs_before):
                g = nc.gpsimd
                reached_apart(pool, ev["norm_max_done"], u1, x_rest, 16)
                g.partition_all_reduce(norm_all[:], norm_max[:], P, bass.bass_isa.ReduceOp.max).then_inc(ev["norm_all_done"], 1)
                reached(pool, ev["norm_all_done"], u1)
                g.tensor_tensor(norm_all[:, 2:3], norm_all[:, 2:3], norm_all[:, 3:4], ALU.add).then_inc(ev["key_min_sum_done"], 1)
                reached(pool, ev["key_min_sum_done"], u1)
                g.tensor_tensor(products[:], norm_all[:, 1:3], norm_all[:, 0:1].broadcast_to([P, 2]), ALU.mult)\
                    .then_inc(ev["products_done"], 1)
                reached(pool, ev["products_done"], u1)
                g.tensor_tensor(bounds_sq[:], products[:], signed_scale[:], ALU.mult).then_inc(ev["bounds_sq_done"], 1)
                reached_apart(pool, ev["bounds_sq_done"], u1, x_rest, 16)
                g.tensor_scalar(bounds_cut[:], bounds_sq[:], 1e-30, 1e30, ALU.max, ALU.min).then_inc(ev["bounds_cut_done"], 1)
                reached(pool, ev["bounds_cut_done"], u1)
                g.tensor_tensor(bounds[:], bounds_cut[:], half[:], ALU.pow).then_inc(ev["bounds_done"], 1)
                reached(pool, ev["bounds_done"], u1)
                g.tensor_tensor(span[:], bounds[:, 0:1], bounds[:, 1:2], ALU.add).then_inc(ev["span_done"], 1)
                g.tensor_scalar(sigma[:], bounds[:, 0:1], MAX_EXP, MAX_EXP, ALU.max, ALU.subtract).then_inc(ev["sigma_done"], 1)
                reached_apart(pool, ev["span_done"], u1, x_rest, 16)
                g.tensor_scalar(bounded_int[:, parity, :], span[:], SPAN_MAX, 1.0, ALU.is_le, ALU.mult)
                g.tensor_scalar(minus_one_if[:], span[:], SPAN_MAX, -1.0, ALU.is_le, ALU.mult).then_inc(ev["bounded_done"], 1)
                reached(pool, ev["sigma_done"], u1)
                reached(pool, ev["bounded_done"], u1)
                if probs_before is not None:
                    reached(pool, probs_ready[KT - 1][G - 1], probs_before)
                g.tensor_tensor(shift[:, parity, :], sigma[:], minus_one_if[:], ALU.mult).then_inc(ev["shift_done"], 1)

            rstd(1, moments1, var_eps1, rstd1, "moments1_done", "var1_done", "rstd1_done")
            norms_of_tile(1, 0, None)
            pool.wait_ge(x_rest, 16)
            rstd(2, moments1, var_eps1, rstd1, "moments1_done", "var1_done", "rstd1_done")
            pool.wait_ge(experts_loaded, 16)
            pool.wait_ge(setup_dve, SETUP_GATES)
            for b in range(B):
                last = nc.gpsimd.tensor_tensor(experts_gated[:, b], experts_in[:],
                                               spread(gates[:, 1, b, :], 1, NE), ALU.mult)
            last.then_inc(experts_are_gated, 1)
            pool.wait_ge(setup_dve, SETUP_ALL)
            pool.wait_ge(x_rest, 16)

            def gated_x(w, w1):
                b = batch_of(pool, w)
                src = x_all[:, w, :] if isinstance(w, int) else x_all[:, bass.ds(w, 1), :]
                bias = bo_gated[:, b, :] if isinstance(w, int) else bo_gated[:, bass.ds(b, 1), :]
                dst = x_gated[:] if isinstance(w, int) else x_gated[:].rearrange("p (a d) -> p a d", a=1)
                nc.gpsimd.tensor_tensor(dst, src, bias, ALU.add).then_inc(ev["x_gated_done"], 1)

            def tile(t, parity, before, after):
                w, u1, v1 = plus(pool, t, -1), plus(pool, t, 2), plus(pool, t, 3)
                if before:
                    gated_x(w, t)
                    rstd(t, moments2, var_eps2, rstd2, "moments2_done", "var2_done", "rstd2_done")
                if after:
                    norms_of_tile(u1, 1 - parity, t if before else None)
                if after == 2:
                    rstd(v1, moments1, var_eps1, rstd1, "moments1_done", "var1_done", "rstd1_done")

            def last():
                gated_x(T - 1, T)
                rstd(T, moments2, var_eps2, rstd2, "moments2_done", "var2_done", "rstd2_done")
            tiles(pool, tile, last)

        @block.scalar
        def _(act):
            act.wait_ge(setup_dve, SETUP_CT)
            nc.scalar.activation(c_exp[:], cT[:], ACT.Exp, scale=-1.0).then_inc(setup_act, 1)

            def router(w1):
                reached(act, ev["logits0_done"], w1)
                nc.scalar.activation(router_exp[:], logits0[:], ACT.Exp, accum_out=router_sum[:]).then_inc(ev["router_exp_done"], 1)

            def tile(t, parity, before, after):
                t1 = plus(act, t, 1)
                reached(act, ev["shift_done"], t1)
                for k in range(KT):
                    for g in range(G):
                        reached(act, scores_ready[k][g], t1)
                        reached(act, pv_done[(k - 2) % KT], t if k < 2 else t1)
                        nc.scalar.activation(probs[:, k % 2, g, :], ps_scores[:, g, :], ACT.Exp,
                                             bias=shift[:, parity, :], scale=SCALE).then_inc(probs_ready[k][g], 1)
                    if k == 5 and before:
                        router(t)
            tiles(act, tile, lambda: router(T))

        @block.tensor
        def _(pe):
            pe.wait_ge(ident_ready, 2)
            pe.wait_ge(w_loaded, 16)
            for k in range(3):
                mm = nc.tensor.transpose(ps_c[:, 0, k * P:(k + 1) * P], wqkv_in[:, k, :], ident[:])
            mm.then_inc(setup_pe, 1)
            pe.wait_ge(small_loaded, 16 * 6)
            nc.tensor.transpose(ps_c[:, 1, 0:B], c_in[:], ident[0:B, 0:B])
            nc.tensor.transpose(ps_c[:, 1, 8:8 + NE], router_in[:], ident[0:NE, 0:NE])
            nc.tensor.transpose(ps_c[:, 1, P:2 * P], wo_in[:], ident[:]).then_inc(setup_pe, 1)
            pe.wait_ge(setup_dve, SETUP_SILU)
            for k, chunk in enumerate((0, 1, 3, 4)):
                mm = nc.tensor.matmul(ps_a[:, k * B:(k + 1) * B], wmod_in[:, chunk * D:(chunk + 1) * D], siluT[:],
                                      start=True, stop=True)
            mm.then_inc(setup_pe, 1)
            for k, chunk in enumerate((2, 5)):
                for b in range(B):
                    mm = nc.tensor.matmul(ps_c[:, k, b * D:(b + 1) * D], silu_wide[:, b, :],
                                          wmod_in[:, chunk * D:(chunk + 1) * D], start=True, stop=True)
            mm.then_inc(setup_pe, 1)

            def a_transpose(u, u1):
                reached(pe, ev["xhat_done"], u1)
                reached(pe, chunk_saved[3], u)
                nc.tensor.transpose(ps_a[:, 0:P], xhat[:], ident[:]).then_inc(ev["xhatT_done"], 1)

            def a_project(u1):
                reached(pe, ev["hT_done"], u1)
                w = wqkvT[:].rearrange("p (j c d) -> p j c d", c=3, d=hd)
                nc.tensor.matmul(ps_a[:, 0:2 * D], hT[:], w[:, :, 0:2, :], start=True, stop=True).then_inc(ev["qk_ps_done"], 1)

            def a_project_v(u1):
                reached(pe, ev["qk_done"], u1)
                wv = wqkvT[:].rearrange("p (k o c d) -> p o k c d", o=2, c=3, d=hd)
                for g in range(G):
                    for odd in range(2):
                        mm = nc.tensor.matmul(ps_a[odd * R:(odd + 1) * R, 2 * D + g * R:2 * D + (g + 1) * R],
                                              hT[:, g * R:(g + 1) * R], wv[:, odd, :, 2, :], start=True, stop=True)
                mm.then_inc(ev["v_ps_done"], 1)

            def a_chunk(u1, ck):
                if ck == 0:
                    reached(pe, ev["k_slots_done"], u1)
                if ck == 2:
                    reached(pe, ev["q_slots_done"], u1)
                if ck == 0:
                    reached(pe, ev["values_done"], u1)
                else:
                    reached(pe, chunk_saved[ck - 1], u1)
                for j in range(8):
                    mm = nc.tensor.transpose(ps_a_b[:, j, :], slots[:, 0 if ck >= 2 else 1, 8 * (ck % 2) + j, :],
                                             ident_b[:])
                mm.then_inc(chunkT_done[ck], 1)

            def m_stage(u, parity, probs_before):
                reached_apart(pe, ev["bounded_done"], plus(pe, u, 1), setup_dve, SETUP_MOD)
                flag = pe.value_load(bounded_int[0:1, parity, :], min_val=0, max_val=1)
                with pe.If(flag == 0):
                    if probs_before is not None:
                        for g in range(G):
                            reached(pe, probs_ready[KT - 1][g], probs_before)
                    scores0, taken0 = plus(pe, u, 0) * M_PE, plus(pe, u, 0) * M_DVE
                    reached(pe, chunk_saved[3], plus(pe, u, 1))
                    for n in range(G * KT):
                        g, k = n // KT, n % KT
                        if n >= 2:
                            reached(pe, m_taken, taken0 + (n - 1))
                        for h in range(2):
                            mm = nc.tensor.matmul(ps_scores[:, n % 2, h * HALF:(h + 1) * HALF],
                                                  query_stack[:, parity, g, 2 * k:2 * k + 2, :].rearrange("p j r -> p (j r)"),
                                                  key_stack[:, parity, g, 8 * h:8 * h + 8, :].rearrange("p j r -> p (j r)"),
                                                  start=True, stop=True)
                        mm.then_inc(m_scores, 1)
                    reached(pe, m_taken, taken0 + (G * KT + 3))
                    for g in range(G):
                        rows = ps_scores[MAX_ROW:MAX_ROW + PARTS, g, 0:HALF].bitcast(BF16)
                        for k in range(KT):
                            mm = nc.tensor.transpose(rows[:, k * P:(k + 1) * P], max_parts[:, g * KT + k, :], ident_b[:],
                                                     tile_position=(0, MAX_ROW))
                        mm.then_inc(m_scores, 1)
                    reached(pe, m_taken, taken0 + M_DVE)
                with pe.Else():
                    pe.sem_inc(m_scores, M_PE)

            def scores(u1, parity, k, probs_before):
                if k == 0:
                    reached(pe, chunk_saved[3], u1)
                for g in range(G):
                    if probs_before is not None:
                        reached(pe, probs_ready[(k - 1) % KT][g], probs_before)
                    for h in range(2):
                        mm = nc.tensor.matmul(ps_scores[:, g, h * HALF:(h + 1) * HALF],
                                              key_stack[:, parity, g, 2 * k:2 * k + 2, :].rearrange("p j r -> p (j r)"),
                                              query_stack[:, parity, g, 8 * h:8 * h + 8, :].rearrange("p j r -> p (j r)"),
                                              start=True, stop=True)
                    mm.then_inc(scores_ready[k][g], 1)

            def weigh(t, t1, parity, k):
                if k == 0:
                    reached(pe, ev["attn_saved"], t)
                    reached(pe, ev["values_done"], t1)
                for g in range(G):
                    reached(pe, probs_ready[k][g], t1)
                    for h in range(2):
                        q = 32 * (2 * g + h)
                        mm = nc.tensor.matmul(ps_attn[q:q + 32, :], values[:, parity, g, k, :],
                                              probs[:, k % 2, g, h * HALF:(h + 1) * HALF],
                                              start=(k == 0), stop=(k == KT - 1), tile_position=(0, q))
                mm.then_inc(pv_done[k], 1)

            def c_attnT(w, w1):
                reached_apart(pe, ev["attn_saved"], w1, setup_dve, SETUP_ALL)
                for half in range(2):
                    for j in range(4):
                        mm = nc.tensor.transpose(ps_c[0:R, half, j * P:(j + 1) * P], attn[:, 4 * half + j, :], ident[:])
                    mm.then_inc(attnT_done[half], 1)

            def c_valsT(w1):
                reached_apart(pe, ev["vals_done"], w1, setup_dve, SETUP_ALL)
                for g in range(G):
                    mm = nc.tensor.transpose(ps_c[:, 0, g * R:(g + 1) * R], vals[:, g, :], ident[0:R, 0:R])
                mm.then_inc(ev["valsT_ps_done"], 1)

            def c_project(w, w1):
                reached(pe, ev["valsT_done"], w1)
                b = batch_of(pe, w)
                rhs = wo_gated[:, b, :] if isinstance(b, int) else wo_gated[:, bass.ds(b, 1), :].rearrange("p a d -> p (a d)")
                nc.tensor.matmul(ps_c[:, 1, 0:D], valsT[:], rhs, start=True, stop=True).then_inc(ev["attn_proj_done"], 1)

            def c_h2T(w1):
                reached(pe, ev["x1hat_done"], w1)
                nc.tensor.transpose(ps_c[:, 0, 0:P], x1hat[:], ident[:]).then_inc(ev["x1hatT_done"], 1)

            def c_logits(w1):
                reached(pe, ev["h2T_done"], w1)
                nc.tensor.matmul(ps_c[:, 1, 0:NE], h2T[:], routerT[:], start=True, stop=True).then_inc(ev["logits_done"], 1)

            def c_experts(w, w1, half):
                if half == 0:
                    reached(pe, ev["h2T_done"], w1)
                    pe.wait_ge(experts_are_gated, 1)
                else:
                    reached(pe, ev["logits0_done"], w1)
                b = batch_of(pe, w)
                e0 = half * NE // 2
                if isinstance(b, int):
                    rhs = experts_gated[:, b, e0:e0 + NE // 2, :].rearrange("p e d -> p (e d)")
                else:
                    rhs = experts_gated[:, bass.ds(b, 1), e0:e0 + NE // 2, :].rearrange("p a e d -> p (a e d)")
                nc.tensor.matmul(ps_c[:, half, :], h2T[:], rhs, start=True, stop=True).then_inc(experts_done[half], 1)

            def tile(t, parity, before, after):
                t1, u1 = plus(pe, t, 1), plus(pe, t, 2)
                w = plus(pe, t, -1)
                for k in range(KT):
                    if k < KT - 1:
                        scores(t1, parity, k + 1, t1)
                    elif after:
                        m_stage(t1, 1 - parity, t1)
                        scores(u1, 1 - parity, 0, t1)
                    if after and k == 0:
                        a_transpose(t1, u1)
                    if before and k == 2:
                        c_project(w, t)
                    if before and k == KT - 1:
                        c_experts(w, t, 1)
                    weigh(t, t1, parity, k)
                    if before and k == 0:
                        c_attnT(w, t)
                    if after and k == 0:
                        a_project(u1)
                    if after and k == 1:
                        a_project_v(u1)
                    if before and k == 1:
                        c_valsT(t)
                    if before and k == 3:
                        c_h2T(t)
                    if before and k == 4:
                        c_logits(t)
                    if before and k == 6:
                        c_experts(w, t, 0)
                    if after and 2 <= k <= 5:
                        a_chunk(u1, k - 2)

            def last():
                w = T - 1
                c_attnT(w, T)
                c_valsT(T)
                c_project(w, T)
                c_h2T(T)
                c_logits(T)
                c_experts(w, T, 0)
                c_experts(w, T, 1)

            pe.wait_ge(setup_dve, SETUP_MOD)
            a_transpose(0, 1)
            a_project(1)
            a_project_v(1)
            for ck in range(4):
                a_chunk(1, ck)
            pe.wait_ge(setup_dve, SETUP_GATES)
            pe.wait_ge(stacks_const, 1)
            m_stage(0, 0, None)
            scores(1, 0, 0, None)
            pe.wait_ge(setup_dve, SETUP_ALL)
            tiles(pe, tile, last)

        @block.vector
        def _(dve):
            v = nc.vector

            def step(ins):
                step.n += 1
                ins.then_inc(setup_dve, 1)
                dve.wait_ge(setup_dve, step.n)
            step.n = 0

            v.memset(slots[:].rearrange("p c j m -> p (c j m)").bitcast(U32), 0)
            v.memset(values[:], 0.0).then_inc(stacks_zero, 1)
            dve.wait_ge(stacks_zero, 1)
            v.memset(values[:, :, :, :, hd:hd + 1], 1.0)
            v.memset(slots[:, 1, :, MAX_ROW:MAX_ROW + PARTS], 1.0).then_inc(stacks_const, 1)

            def a_moments(u, u1):
                src = x_all[:, u, :] if isinstance(u, int) else x_all[:, bass.ds(u, 1), :]
                v.bn_stats(stats1[:], src).then_inc(ev["stats1_done"], 1)
                reached_apart(dve, ev["stats1_done"], u1, x_rest, 16)
                v.bn_aggr(moments1[:], stats1[:]).then_inc(ev["moments1_done"], 1)

            def a_xhat(u, u1):
                reached(dve, ev["rstd1_done"], u1)
                reached(dve, ev["moments1_done"], u1)
                src = x_all[:, u, :] if isinstance(u, int) else x_all[:, bass.ds(u, 1), :]
                dst = xhat[:] if isinstance(u, int) else xhat[:].rearrange("p (a d) -> p a d", a=1)
                v.tensor_scalar(dst, src, moments1[:, 0:1], rstd1[:], ALU.subtract, ALU.mult).then_inc(ev["xhat_done"], 1)

            def mod_col(u, k):
                return mod_tab[:, u, k:k + 1] if isinstance(u, int) else \
                    mod_tab[:, bass.ds(u, 1), k:k + 1].rearrange("p a k -> p (a k)")

            def a_hT(u, u1):
                reached(dve, ev["xhatT_done"], u1)
                v.tensor_scalar(hT[:], ps_a[:, 0:P], mod_col(u, 1), mod_col(u, 0), ALU.mult, ALU.add).then_inc(ev["hT_done"], 1)

            def a_split(u1):
                reached(dve, ev["qk_ps_done"], u1)
                bias = bqkv_rows[:].rearrange("p (j c d) -> p c j d", c=3, d=hd)
                v.tensor_tensor(qk[:], ps_a[:, 0:2 * D].rearrange("p (j c d) -> p c j d", j=J, c=2), bias[:, 0:2],
                                ALU.add).then_inc(ev["qk_done"], 1)
                part = [parts[:, :, :, a, :].rearrange("p c j d -> p (c j) d") for a in range(PARTS)]
                q = qk[:].rearrange("p c j d -> p (c j) d")
                rest = qk_rest[:].rearrange("p c j d -> p (c j) d")
                reached(dve, ev["qk_done"], u1)
                v.tensor_copy(part[0], q).then_inc(ev["hi_done"], 1)
                reached(dve, ev["hi_done"], u1)
                v.tensor_tensor(rest, q, part[0], ALU.subtract).then_inc(ev["rest1_done"], 1)
                reached(dve, ev["rest1_done"], u1)
                v.tensor_copy(part[1], rest).then_inc(ev["mid_done"], 1)
                reached(dve, ev["mid_done"], u1)
                v.tensor_tensor(part[2], rest, part[1], ALU.subtract).then_inc(ev["parts_done"], 1)

            def a_values(u1, parity):
                reached(dve, ev["v_ps_done"], u1)
                v.tensor_tensor(values[:, parity, :, :, 0:hd],
                                ps_a[:, 2 * D:2 * D + G * R].rearrange("p (g k d) -> p g k d", g=G, d=hd),
                                spread(bv[:], 1, G),
                                ALU.add).then_inc(ev["values_done"], 1)

            def a_slots(u1):
                reached(dve, ev["parts_done"], u1)
                v.tensor_copy(slots[:, 1, :, 0:SLOTS].rearrange("p j (a m) -> p j a m", a=PARTS),
                              spread(parts[:, 1].rearrange("p j b d -> p j (b d)"), 2, PARTS)).then_inc(ev["k_slots_done"], 1)
                v.tensor_copy(slots[:, 0, :, 0:SLOTS].rearrange("p j (a b d) -> p j a b d", a=PARTS, b=PARTS),
                              spread(parts[:, 0], 3, PARTS)).then_inc(ev["q_slots_done"], 1)

            def a_norms(u1):
                flat = squares[:].rearrange("p c j d -> p (c j d)")
                src = qk[:].rearrange("p c j d -> p (c j d)")
                v.tensor_tensor(flat, src, src, ALU.mult).then_inc(ev["squares_done"], 1)
                reached(dve, ev["squares_done"], u1)
                v.tensor_reduce(norms[:], squares[:].rearrange("p c j d -> p (c j) d"), AX.X, ALU.add)\
                    .then_inc(ev["norms_done"], 1)
                reached(dve, ev["norms_done"], u1)
                v.tensor_reduce(key_min[:], norms[:, J:2 * J], AX.X, ALU.min).then_inc(ev["key_min_done"], 1)
                v.tensor_reduce(norm_max[:, 0:2], norms[:].rearrange("p (c j) -> p c j", c=2), AX.X, ALU.max)
                reached(dve, ev["key_min_done"], u1)
                v.tensor_scalar(norm_max[:, 2:2 + G], head_far[:], key_min[:], None, ALU.subtract)\
                    .then_inc(ev["norm_max_done"], 1)

            def a_save_chunk(u1, parity, ck, scores_before):
                reached(dve, chunkT_done[ck], u1)
                if ck == 0 and scores_before is not None:
                    reached(dve, scores_ready[KT - 1][G - 1], scores_before)
                v.tensor_copy(shape_chunk(ck, parity), ps_a_b.rearrange("p j (g r) -> p j g r", g=G))\
                    .then_inc(chunk_saved[ck], 1)

            def load_bounded(u1, parity):
                reached_apart(dve, ev["bounded_done"], u1, x_rest, 16)
                return dve.value_load(bounded_int[0:1, parity, :], min_val=0, max_val=1)

            def m_stage(u, parity, is_bounded):
                with dve.If(is_bounded == 0):
                    scores0, taken0 = plus(dve, u, 0) * M_PE, plus(dve, u, 0) * M_DVE
                    for n in range(G * KT):
                        reached(dve, m_scores, scores0 + (n + 1))
                        v.tensor_reduce(row_max[:, n:n + 1], ps_scores[:, n % 2, :], AX.X, ALU.max).then_inc(m_taken, 1)
                    reached(dve, m_taken, taken0 + G * KT)
                    v.tensor_scalar(max_parts[:, :, 0], row_max[:], -1.0, None, ALU.mult)
                    v.tensor_scalar(max_rest[:], row_max[:], -1.0, None, ALU.mult).then_inc(m_taken, 1)
                    reached(dve, m_taken, taken0 + (G * KT + 1))
                    v.tensor_tensor(max_rest2[:], max_rest[:], max_parts[:, :, 0], ALU.subtract)
                    v.tensor_tensor(max_parts[:, :, 1], max_rest[:], max_parts[:, :, 0], ALU.subtract).then_inc(m_taken, 1)
                    reached(dve, m_taken, taken0 + (G * KT + 2))
                    v.tensor_tensor(max_parts[:, :, 2], max_rest2[:], max_parts[:, :, 1], ALU.subtract).then_inc(m_taken, 1)
                    for g in range(G):
                        reached(dve, m_scores, scores0 + (G * KT + 1 + g))
                        v.tensor_copy(query_stack[MAX_ROW:MAX_ROW + PARTS, parity, g].rearrange("p j r -> p (j r)"),
                                      ps_scores[MAX_ROW:MAX_ROW + PARTS, g, 0:HALF].bitcast(BF16)).then_inc(m_taken, 1)
                with dve.Else():
                    dve.sem_inc(m_taken, M_DVE)

            def c_save(w1):
                reached(dve, pv_done[KT - 1], w1)
                v.tensor_copy(attn[:].rearrange("p j r -> p (j r)"), ps_attn[:]).then_inc(ev["attn_saved"], 1)

            def c_vals(w, w1):
                for half in range(2):
                    reached(dve, attnT_done[half], w1)
                    ps = ps_c[0:R, half, :].rearrange("p (j c m) -> p j c m", j=4, c=4)
                    inv = sums_inv[:, 4 * half:4 * half + 4, :]
                    v.reciprocal(inv, ps[:, :, :, hd]).then_inc(ev[f"sums_inv{half}"], 1)
                for half in range(2):
                    reached(dve, ev[f"sums_inv{half}"], w1)
                    ps = ps_c[0:R, half, :].rearrange("p (j c m) -> p j c m", j=4, c=4)
                    inv = sums_inv[:, 4 * half:4 * half + 4, :]
                    dst = vals[:].rearrange("p g (h j d) -> p j (g h) d", h=2, d=hd)[:, 4 * half:4 * half + 4]
                    ins = v.tensor_tensor(dst, ps[:, :, :, 0:hd],
                                          spread(inv, 3, hd), ALU.mult)
                ins.then_inc(ev["vals_done"], 1)

            def c_valsT(w1):
                reached(dve, ev["valsT_ps_done"], w1)
                v.tensor_copy(valsT[:], ps_c[:, 0, 0:P]).then_inc(ev["valsT_done"], 1)

            def c_x1(w1):
                reached(dve, ev["attn_proj_done"], w1)
                reached(dve, ev["x_gated_done"], w1)
                v.tensor_tensor(x1[:], ps_c[:, 1, 0:D], x_gated[:], ALU.add).then_inc(ev["x1_done"], 1)
                reached(dve, ev["x1_done"], w1)
                v.bn_stats(stats2[:], x1[:]).then_inc(ev["stats2_done"], 1)
                reached_apart(dve, ev["stats2_done"], w1, x_rest, 16)
                v.bn_aggr(moments2[:], stats2[:]).then_inc(ev["moments2_done"], 1)

            def c_x1hat(w1):
                reached(dve, ev["rstd2_done"], w1)
                reached(dve, ev["moments2_done"], w1)
                v.tensor_scalar(x1hat[:], x1[:], moments2[:, 0:1], rstd2[:], ALU.subtract, ALU.mult)\
                    .then_inc(ev["x1hat_done"], 1)

            def c_h2T(w, w1):
                reached(dve, ev["x1hatT_done"], w1)
                v.tensor_scalar(h2T[:], ps_c[:, 0, 0:P], mod_col(w, 3), mod_col(w, 2), ALU.mult, ALU.add)\
                    .then_inc(ev["h2T_done"], 1)

            def c_logits(w1):
                reached_apart(dve, ev["logits_done"], w1, x_rest, 16)
                v.max(top_logits[:], ps_c[:, 1, 0:NE]).then_inc(ev["top_logits_done"], 1)
                reached(dve, ev["top_logits_done"], w1)
                v.tensor_scalar(logits0[:], ps_c[:, 1, 0:NE], top_logits[:, 0:1], None, ALU.subtract)\
                    .then_inc(ev["logits0_done"], 1)

            def c_router_top(w1):
                reached(dve, ev["router_exp_done"], w1)
                v.reciprocal(router_inv[:], router_sum[:]).then_inc(ev["router_inv_done"], 1)
                reached(dve, ev["router_inv_done"], w1)
                v.tensor_scalar(router_p[:], router_exp[:], router_inv[:], None, ALU.mult).then_inc(ev["router_p_done"], 1)
                reached_apart(dve, ev["router_p_done"], w1, x_rest, 16)
                v.max(top_p[:], router_p[:]).then_inc(ev["top_p_done"], 1)
                reached_apart(dve, ev["top_p_done"], w1, x_rest, 16)
                v.max_index(top_id[:], top_p[:], router_p[:]).then_inc(ev["top_id_done"], 1)
                v.tensor_tensor(pair_sum[:], top_p[:, 0:1], top_p[:, 1:2], ALU.add).then_inc(ev["pair_sum_done"], 1)
                reached(dve, ev["top_id_done"], w1)
                v.tensor_copy(top_idf[:], top_id[:]).then_inc(ev["top_idf_done"], 1)
                reached(dve, ev["pair_sum_done"], w1)
                v.tensor_scalar(pair_eps[:], pair_sum[:], TOP_EPS, None, ALU.add).then_inc(ev["pair_eps_done"], 1)

            def c_router_weights(w1):
                reached(dve, ev["pair_eps_done"], w1)
                v.reciprocal(pair_inv[:], pair_eps[:]).then_inc(ev["pair_inv_done"], 1)
                reached(dve, ev["pair_inv_done"], w1)
                v.tensor_scalar(pair_w[:], top_p[:, 0:2], pair_inv[:], None, ALU.mult).then_inc(ev["pair_w_done"], 1)
                reached(dve, ev["pair_w_done"], w1)
                reached(dve, ev["top_idf_done"], w1)
                v.tensor_scalar(coef0[:], expert_ids[:], top_idf[:, 0:1], pair_w[:, 0:1], ALU.is_equal, ALU.mult)\
                    .then_inc(ev["coef0_done"], 1)
                v.tensor_scalar(coef1[:], expert_ids[:], top_idf[:, 1:2], pair_w[:, 1:2], ALU.is_equal, ALU.mult)\
                    .then_inc(ev["coef1_done"], 1)
                v.tensor_tensor(pair_pw[:], top_p[:, 0:2], pair_w[:], ALU.mult).then_inc(ev["pair_pw_done"], 1)
                reached(dve, ev["pair_pw_done"], w1)
                v.tensor_tensor(bias_w[:], pair_pw[:, 0:1], pair_pw[:, 1:2], ALU.add).then_inc(ev["bias_w_done"], 1)
                reached(dve, ev["coef0_done"], w1)
                reached(dve, ev["coef1_done"], w1)
                v.tensor_tensor(coef[:], coef0[:], coef1[:], ALU.add).then_inc(ev["coef_done"], 1)

            def c_weigh(w, w1):
                b = batch_of(dve, w)
                reached(dve, ev["bias_w_done"], w1)
                gate = gates[:, 1, b, :] if isinstance(b, int) else \
                    gates[:, 1, bass.ds(b, 1), :].rearrange("p a d -> p (a d)")
                v.scalar_tensor_tensor(out=base[:], in0=gate, scalar=bias_w[:], in1=x1[:], op0=ALU.mult,
                                       op1=ALU.add).then_inc(ev["base_done"], 1)
                reached(dve, experts_done[1], w1)
                reached(dve, ev["coef_done"], w1)
                v.tensor_tensor(weighted[:], ps_c[:].rearrange("p h (e d) -> p (h e) d", d=D),
                                spread(coef[:], 2, D), ALU.mult)\
                    .then_inc(ev["weighted_done"], 1)

            def c_mix(w, w1):
                reached(dve, ev["weighted_done"], w1)
                v.tensor_reduce(mixed[:], weighted[:].rearrange("p e d -> p d e"), AX.X, ALU.add)\
                    .then_inc(ev["mixed_done"], 1)
                reached(dve, ev["mixed_done"], w1)
                reached(dve, ev["base_done"], w1)
                if isinstance(w, int):
                    v.tensor_tensor(out_all[:, w, :], base[:], mixed[:], ALU.add).then_inc(ev["out_done"], 1)
                else:
                    v.tensor_tensor(out_all[:, bass.ds(w, 1), :], base[:].rearrange("p (a d) -> p a d", a=1),
                                    mixed[:].rearrange("p (a d) -> p a d", a=1), ALU.add).then_inc(ev["out_done"], 1)

            def tile(t, parity, before, after):
                u, u1, w = plus(dve, t, 1), plus(dve, t, 2), plus(dve, t, -1)
                nn, nn1 = plus(dve, t, 2), plus(dve, t, 3)
                other = 1 - parity
                if before:
                    c_save(t)
                if before == 2:
                    c_mix(plus(dve, t, -2), w)
                if after:
                    a_hT(u, u1)
                if before:
                    c_vals(w, t)
                if after:
                    a_split(u1)
                if before:
                    c_valsT(t)
                if after:
                    a_values(u1, other)
                    a_slots(u1)
                if before:
                    c_x1(t)
                if after:
                    a_norms(u1)
                    a_save_chunk(u1, other, 0, t)
                if before:
                    c_x1hat(t)
                    c_h2T(w, t)
                if after:
                    a_save_chunk(u1, other, 1, None)
                if before:
                    c_logits(t)
                if after == 2:
                    a_moments(nn, nn1)
                if after:
                    a_save_chunk(u1, other, 2, None)
                    is_bounded = load_bounded(u1, other)
                if before:
                    c_router_top(t)
                if after == 2:
                    a_xhat(nn, nn1)
                if after:
                    a_save_chunk(u1, other, 3, None)
                if before:
                    c_router_weights(t)
                if after:
                    m_stage(u, other, is_bounded)
                if before:
                    c_weigh(w, t)

            def last():
                w = T - 1
                c_save(T)
                c_mix(T - 2, T - 1)
                c_vals(w, T)
                c_valsT(T)
                c_x1(T)
                c_x1hat(T)
                c_h2T(w, T)
                c_logits(T)
                c_router_top(T)
                c_router_weights(T)
                c_weigh(w, T)
                c_mix(w, T)

            dve.wait_ge(x_first, 16)
            a_moments(0, 1)
            dve.wait_ge(small_loaded, 16 * 6)
            dve.wait_ge(setup_pe, 1)
            step(v.tensor_copy(wqkvT[:], ps_c[:, 0, 0:3 * D]))
            dve.wait_ge(setup_pe, 2)
            step(v.tensor_copy(cT[:], ps_c[:, 1, 0:B]))
            assert step.n == SETUP_CT
            step(v.tensor_copy(routerT[:], ps_c[:, 1, 8:8 + NE]))
            step(v.tensor_copy(woT[:], ps_c[:, 1, P:2 * P]))
            dve.wait_ge(setup_act, 1)
            step(v.tensor_scalar(c_exp1[:], c_exp[:], 1.0, None, ALU.add))
            step(v.reciprocal(c_sig[:], c_exp1[:]))
            step(v.tensor_tensor(siluT[:], cT[:], c_sig[:], ALU.mult))
            step(v.tensor_copy(silu_wide[:], spread(siluT[:], 2, P)))
            assert step.n == SETUP_SILU
            bq = bqkv_rows[:].rearrange("p (k o c d) -> p o k c d", o=2, c=3, d=hd)
            for odd in range(2):
                v.tensor_copy(bv[odd * R:(odd + 1) * R], bq[odd * R:(odd + 1) * R, odd, :, 2, :])
            dve.wait_ge(setup_pe, 3)
            for k in range(4):
                dst = mod_tab[:].rearrange("p (b i) k -> p b i k", i=TB)[:, :, :, k]
                src = spread(ps_a[:, k * B:(k + 1) * B], 2, TB)
                if k % 2:
                    ins = v.tensor_scalar(dst, src, 1.0, None, ALU.add)
                else:
                    ins = v.tensor_copy(dst, src)
            step(ins)
            assert step.n == SETUP_MOD
            dve.wait_ge(setup_pe, 4)
            g_ps = ps_c[:].rearrange("p a (b d) -> p a b d", d=D)
            step(v.tensor_scalar(gate_flag[:], g_ps, 0.0, 2.0, ALU.is_ge, ALU.mult))
            step(v.tensor_scalar(gate_sign[:], gate_flag[:], -1.0, None, ALU.add))
            step(v.tensor_tensor(gate_size[:], g_ps, gate_sign[:], ALU.mult))
            step(v.scalar_tensor_tensor(out=gates[:].rearrange("p a b d -> p (a b d)"),
                                        in0=gate_size[:].rearrange("p a b d -> p (a b d)"), scalar=GATE_MIN,
                                        in1=gate_sign[:].rearrange("p a b d -> p (a b d)"), op0=ALU.max, op1=ALU.mult))
            assert step.n == SETUP_GATES
            v.tensor_tensor(wo_gated[:], spread(woT[:], 1, B), gates[:, 0], ALU.mult)
            step(v.tensor_tensor(bo_gated[:], spread(bo_rows[:], 1, B), gates[:, 0],
                                 ALU.mult))
            a_xhat(0, 1)
            a_hT(0, 1)
            a_split(1)
            a_values(1, 0)
            a_slots(1)
            dve.wait_ge(pool_consts, 1 + G)
            a_norms(1)
            for ck in range(4):
                a_save_chunk(1, 0, ck, None)
            m_stage(0, 0, load_bounded(1, 0))
            dve.wait_ge(x_rest, 16)
            a_moments(1, 2)
            a_xhat(1, 2)
            tiles(dve, tile, last)


_INS = ["L0_attn_x", "L0_attn_Wqkv", "L0_attn_bqkv", "L0_attn_Wo", "L0_attn_bo", "L0_ffn_router_w",
        "L0_ffn_expert_weights", "L0_c", "L0_wmod"]
_OUTS = [((4, 1024, 128), "float32")]


def kernel(**inputs):
    import numpy as _np
    import concourse.bacc as _bacc
    from concourse import mybir as _mybir
    from concourse.bass_utils import run_bass_kernel_spmd as _run

    nc = _bacc.Bacc("TRN2", target_bir_lowering=False, num_devices=1)
    arrays, args = {}, []
    for name in _INS:
        a = _np.ascontiguousarray(inputs[name])
        arrays[f"in_{name}_dram"] = a
        args.append(nc.dram_tensor(f"in_{name}_dram", a.shape, _mybir.dt.from_np(a.dtype), kind="ExternalInput").ap())
    for i, (shape, dtype) in enumerate(_OUTS):
        dt = _mybir.dt.from_np(_np.dtype(dtype))
        args.append(nc.dram_tensor(f"out_{i}_dram", shape, dt, kind="ExternalOutput").ap())
    adaln_block(nc, *args)
    r = _run(nc, [arrays], core_ids=[0])
    got = tuple(r.results[0][f"out_{i}_dram"] for i in range(len(_OUTS)))
    return got[0]
```

```python
from contextlib import ExitStack

import concourse.bass as bass
from concourse import mybir

ALU = mybir.AluOpType
ACT = mybir.ActivationFunctionType
AX = mybir.AxisListType
F32 = mybir.dt.float32
BF16 = mybir.dt.bfloat16
U32 = mybir.dt.uint32
I32 = mybir.dt.int32

P = 128
HEADS = 16
PARTS = 3
EPS = 1e-5
TOP_EPS = 1e-6
GATE_MIN = 0.25
MAX_EXP = 30.0
SPAN_MAX = 90.0
FAR = -1e30
MAX_ROW = 96

SETUP_CT, SETUP_SILU, SETUP_WQKV, SETUP_MOD, SETUP_COLUMNS, SETUP_ALL = 1, 4, 5, 6, 10, 11


def reached(eng, sem, count):
    if not isinstance(count, int) or count > 0:
        eng.wait_ge(sem, count)


def reached_apart(eng, sem, count, past, past_count):
    if not isinstance(count, int):
        count = eng.to_reg(count)
        eng.wait_ge(past, past_count)
    reached(eng, sem, count)


def spread(ap, axis, n):
    ap = ap.unsqueeze(axis)
    shape = list(ap.shape)
    shape[axis] = n
    return ap.broadcast_to(shape)


def adaln_block(nc, x, Wqkv, bqkv, Wo, bo, router_w, expert_w, c, wmod, out):
    B, S, D = x.shape
    hd = D // HEADS
    J = HEADS
    R = S // HEADS
    G = P // R
    T = B * S // P
    TB = S // P
    NE = router_w.shape[0]
    TOK = R * J
    KT = TOK // P
    HALF = TOK // 2
    SLOTS = PARTS * PARTS * hd
    SCALE = float(hd) ** -0.5
    assert D == P and hd == 8 and G == 2 and HALF == 512 and T % 2 == 0

    x_tiles = x.rearrange("b s d -> (b s) d").rearrange("(t p) d -> p t d", p=P)
    out_tiles = out.rearrange("b s d -> (b s) d").rearrange("(t p) d -> t p d", p=P)

    with ExitStack() as ctx:
        def sb(name, shape, dt=F32):
            return ctx.enter_context(nc.sbuf_tensor(name, shape, dt))

        def sem(name):
            return ctx.enter_context(nc.semaphore(name))

        x_all = sb("x_all", [P, T, D])
        out_all = sb("out_all", [P, T, D])
        ident = sb("ident", [P, P])
        ident_b = sb("ident_b", [P, P], BF16)
        wqkv_in = sb("wqkv_in", [P, 3, D])
        wo_in = sb("wo_in", [P, D])
        router_in = sb("router_in", [NE, D])
        c_in = sb("c_in", [B, D])
        wmod_in = sb("wmod_in", [P, 6 * D])
        experts_in = sb("experts_in", [P, NE, D])
        bqkv_rows = sb("bqkv_rows", [P, 3 * D])
        bo_rows = sb("bo_rows", [P, D])
        wqkvT = sb("wqkvT", [P, 3 * D])
        wo_perm = sb("wo_perm", [P, 2, R])
        woT = sb("woT", [R, 2, D])
        routerT = sb("routerT", [P, NE])
        cT = sb("cT", [P, B])
        c_exp = sb("c_exp", [P, B])
        c_exp1 = sb("c_exp1", [P, B])
        c_sig = sb("c_sig", [P, B])
        siluT = sb("siluT", [P, B])
        mod_tab = sb("mod_tab", [P, T, 4])
        gate_flag = sb("gate_flag", [P, 2 * B])
        gate_sign = sb("gate_sign", [P, 2 * B])
        gate_size = sb("gate_size", [P, 2 * B])
        gate_cols = sb("gate_cols", [P, 2 * B])
        gates = sb("gates", [P, B, D])
        wo_gated = sb("wo_gated", [R, 2, B, D])
        bo_gated = sb("bo_gated", [P, B, D])
        experts_gated = sb("experts_gated", [P, B, NE, D])
        bv = sb("bv", [P, KT, hd])
        expert_ids = sb("expert_ids", [P, NE])
        minus_half = sb("minus_half", [P, 1])

        stats1 = sb("stats1", [P, 6])
        moments1 = sb("moments1", [P, 2])
        var_eps1 = sb("var_eps1", [P, 1])
        rstd1 = sb("rstd1", [P, 1])
        xhat = sb("xhat", [P, D])
        hT = sb("hT", [P, P])
        qk = sb("qk", [P, 2, J, hd])
        qk_rest = sb("qk_rest", [P, 2, J, hd])
        parts = sb("parts", [P, 2, J, PARTS, hd], BF16)
        slots = sb("slots", [P, 2, J, P], BF16)
        squares = sb("squares", [P, 2, J, hd])
        norms = sb("norms", [P, J * 2])
        key_min = sb("key_min", [P, 1])
        head_far = sb("head_far", [P, G])
        norm_max = sb("norm_max", [P, 2 + G])
        norm_all = sb("norm_all", [P, 2 + G])
        products = sb("products", [P, 2])
        bounds_sq = sb("bounds_sq", [P, 2])
        bounds_cut = sb("bounds_cut", [P, 2])
        bounds = sb("bounds", [P, 2])
        signed_scale = sb("signed_scale", [P, 2])
        half = sb("half", [P, 2])
        span = sb("span", [P, 1])
        sigma = sb("sigma", [P, 1])
        minus_one_if = sb("minus_one_if", [P, 1])
        bounded_int = sb("bounded_int", [P, 2, 1], I32)
        shift = sb("shift", [P, 2, 1])
        key_stack = sb("key_stack", [P, 2, G, J, R], BF16)
        query_stack = sb("query_stack", [P, 2, G, J, R], BF16)
        values = sb("values", [P, 2, G, KT, 32])
        row_max = sb("row_max", [P, G * KT])
        max_rest = sb("max_rest", [P, G * KT])
        max_rest2 = sb("max_rest2", [P, G * KT])
        max_parts = sb("max_parts", [P, G * KT, PARTS], BF16)

        probs = sb("probs", [P, 2, G, TOK])
        attn = sb("attn", [P, 8, R])
        sums_inv = sb("sums_inv", [P, 4, 4])
        vals = sb("vals", [P, G, R])
        valsT = sb("valsT", [R, 2, P])
        x_gated = sb("x_gated", [P, D])
        x1 = sb("x1", [P, D])
        stats2 = sb("stats2", [P, 6])
        moments2 = sb("moments2", [P, 2])
        var_eps2 = sb("var_eps2", [P, 1])
        rstd2 = sb("rstd2", [P, 1])
        x1hat = sb("x1hat", [P, D])
        h2T = sb("h2T", [P, P])
        top_logits = sb("top_logits", [P, 8])
        logits0 = sb("logits0", [P, NE])
        router_exp = sb("router_exp", [P, NE])
        router_sum = sb("router_sum", [P, 1])
        router_inv = sb("router_inv", [P, 1])
        router_p = sb("router_p", [P, NE])
        top_p = sb("top_p", [P, 8])
        top_id = sb("top_id", [P, 8], U32)
        top_idf = sb("top_idf", [P, 8])
        pair_sum = sb("pair_sum", [P, 1])
        pair_eps = sb("pair_eps", [P, 1])
        pair_inv = sb("pair_inv", [P, 1])
        pair_w = sb("pair_w", [P, 2])
        pair_pw = sb("pair_pw", [P, 2])
        bias_w = sb("bias_w", [P, 1])
        coef0 = sb("coef0", [P, NE])
        coef1 = sb("coef1", [P, NE])
        coef = sb("coef", [P, NE])
        weighted = sb("weighted", [P, NE, D])
        mixed = sb("mixed", [P, D])
        base = sb("base", [P, D])

        ps_scores = ctx.enter_context(nc.psum_tensor("ps_scores", [P, G, TOK], F32))
        ps_attn = ctx.enter_context(nc.psum_tensor("ps_attn", [P, 512], F32))
        ps_a = ctx.enter_context(nc.psum_tensor("ps_a", [P, 512], F32))
        ps_c = ctx.enter_context(nc.psum_tensor("ps_c", [P, 2, 512], F32))
        ps_a_b = ps_a[:].bitcast(BF16).rearrange("p (j r) -> p j r", r=P)

        ps_first = [ps_scores[:, ck // 2, (ck % 2) * HALF:(ck % 2 + 1) * HALF].bitcast(BF16)
                    .rearrange("p (j r) -> p j r", r=P) for ck in range(4)]

        x_first, x_rest, c_loaded, wmod_loaded, w_loaded, bqkv_loaded, small_loaded, experts_loaded = (
            sem("x_first"), sem("x_rest"), sem("c_loaded"), sem("wmod_loaded"), sem("w_loaded"), sem("bqkv_loaded"),
            sem("small_loaded"), sem("experts_loaded"))
        out_stored = sem("out_stored")
        ident0, ident_ready, pool_consts, stacks_zero, stacks_const = (
            sem("ident0"), sem("ident_ready"), sem("pool_consts"), sem("stacks_zero"), sem("stacks_const"))
        setup_dve, setup_pe, setup_act, bv_ready, wo_permuted = sem("setup_dve"), sem("setup_pe"), sem("setup_act"), sem("bv_ready"), sem("wo_permuted")
        experts_are_gated = sem("experts_are_gated")
        names = """
            stats1_done moments1_done var1_done rstd1_done xhat_done xhatT_done hT_done qk_ps_done v_ps_done
            qk_done values_done hi_done rest1_done mid_done rest2_done parts_done
            squares_done norms_done key_min_done norm_max_done norm_all_done
            key_min_sum_done products_done bounds_sq_done bounds_cut_done bounds_done span_done sigma_done bounded_done
            shift_done k_slots_done q_slots_done
            attn_saved attnT_done sums_inv_done vals_done valsT_ps_done valsT_done attn_proj_done x_gated_done x1_done
            stats2_done moments2_done var2_done rstd2_done x1hat_done x1hatT_done h2T_done logits_done
            top_logits_done logits0_done router_exp_done router_inv_done router_p_done top_p_done top_id_done
            top_idf_done pair_sum_done pair_eps_done pair_inv_done pair_w_done pair_pw_done bias_w_done
            coef0_done coef1_done coef_done
            base_done weighted_done mixed_done out_done
        """.split()
        ev = {n: sem(n) for n in names}
        scores_ready = [[sem(f"scores_ready_{k}_{g}") for g in range(G)] for k in range(KT)]
        probs_ready = [[sem(f"probs_ready_{k}_{g}") for g in range(G)] for k in range(KT)]
        pv_done = [sem(f"pv_done_{k}") for k in range(KT)]
        chunkT_done = [sem(f"chunkT_done_{k}") for k in range(4)]
        chunk_saved = [sem(f"chunk_saved_{k}") for k in range(4)]
        experts_done = [sem(f"experts_done_{k}") for k in range(2)]
        M_PE, M_DVE = G * KT + G, G * KT + 3 + G
        m_scores, m_taken = sem("m_scores"), sem("m_taken")

        def shape_chunk(c, parity):
            stack = key_stack if c < 2 else query_stack
            j0 = 8 * (c % 2)
            return stack[:, parity, :, j0:j0 + 8, :].rearrange("p g j r -> p j g r")

        def tiles(eng, tile, last):
            tile(0, 0, before=0, after=2)
            tile(1, 1, before=1, after=2)
            with eng.Fori(2, T - 2, 2) as i:
                even = nc.s_assert_within(i, 2, T - 4, skip_runtime_bounds_check_because="i goes up by twos from 2")
                tile(even, 0, before=2, after=2)
                tile(even + 1, 1, before=2, after=2)
            tile(T - 2, 0, before=2, after=1)
            tile(T - 1, 1, before=2, after=0)
            last()

        def plus(eng, t, n):
            return t + n if isinstance(t, int) else eng.snap(t + n)

        def batch_of(eng, t):
            return t // TB if isinstance(t, int) else eng.snap(t // TB, min_val=0, max_val=B - 1)

        block = ctx.enter_context(nc.Block())

        @block.sync
        def _(sp):
            sp.dma_start(c_in[:], c).then_inc(c_loaded, 16)
            sp.dma_start(x_all[:, 0:1, :], x_tiles[:, 0:1, :]).then_inc(x_first, 16)
            sp.dma_start(wqkv_in[:], Wqkv.rearrange("(k p) i -> p k i", p=P)).then_inc(w_loaded, 16)
            sp.dma_start(wmod_in[:], wmod).then_inc(wmod_loaded, 16)
            sp.dma_start(bqkv_rows[:], bqkv.partition_broadcast(P)).then_inc(bqkv_loaded, 16)
            sp.dma_start(wo_in[:], Wo).then_inc(small_loaded, 16)
            sp.dma_start(router_in[:], router_w).then_inc(small_loaded, 16)
            sp.dma_start(bo_rows[:], bo.partition_broadcast(P)).then_inc(small_loaded, 16)
            sp.dma_start(x_all[:, 1:T, :], x_tiles[:, 1:T, :]).then_inc(x_rest, 16)
            sp.dma_start(experts_in[:], expert_w.rearrange("e h o -> h e o")).then_inc(experts_loaded, 16)

            def store(w):
                reached(sp, ev["out_done"], plus(sp, w, 1))
                src = out_all[:, w, :] if isinstance(w, int) else out_all[:, bass.ds(w, 1), :]
                dst = out_tiles[w] if isinstance(w, int) else out_tiles[bass.ds(w, 1)]
                if isinstance(w, int):
                    sp.dma_start(dst, src).then_inc(out_stored, 16)
                else:
                    sp.dma_start(dst.rearrange("t p d -> p t d"), src).then_inc(out_stored, 16)

            def tile(t, parity, before, after):
                if before == 2:
                    store(plus(sp, t, -2))

            def last():
                store(T - 2)
                store(T - 1)
            tiles(sp, tile, last)
            sp.wait_ge(out_stored, 16 * T)

        @block.gpsimd
        def _(pool):
            nc.gpsimd.memset(ident[:], 0.0).then_inc(ident0, 1)
            pool.wait_ge(ident0, 1)
            nc.gpsimd.affine_select(out=ident[:], in_=ident[:], compare_op=ALU.not_equal, fill=1.0, base=0,
                                    pattern=[[-1, P]], channel_multiplier=1).then_inc(ident_ready, 1)
            pool.wait_ge(ident_ready, 1)
            nc.gpsimd.tensor_copy(ident_b[:], ident[:]).then_inc(ident_ready, 1)
            for e in range(NE):
                nc.gpsimd.memset(expert_ids[:, e:e + 1], float(e))
            for g in range(G):
                nc.gpsimd.memset(head_far[:, g:g + 1], FAR)
            for n in range(2):
                nc.gpsimd.memset(signed_scale[:, n:n + 1], (1 - 2 * n) * SCALE * SCALE)
            nc.gpsimd.memset(half[:], 0.5)
            nc.gpsimd.memset(minus_half[:], -0.5).then_inc(pool_consts, 1)
            pool.wait_ge(pool_consts, 1)
            for g in range(G):
                nc.gpsimd.memset(head_far[g * R:(g + 1) * R, g:g + 1], 0.0).then_inc(pool_consts, 1)
                pool.wait_ge(pool_consts, 2 + g)

            def rstd(u1, stats, var_eps, out_, done_in, done_var, done_out):
                reached_apart(pool, ev[done_in], u1, x_rest, 16)
                nc.gpsimd.tensor_scalar(var_eps[:], stats[:, 1:2], EPS, 1.0, ALU.add, ALU.mult).then_inc(ev[done_var], 1)
                reached(pool, ev[done_var], u1)
                nc.gpsimd.tensor_tensor(out_[:], var_eps[:], minus_half[:], ALU.pow).then_inc(ev[done_out], 1)

            def norms_of_tile(u1, parity, probs_before):
                g = nc.gpsimd
                reached_apart(pool, ev["norm_max_done"], u1, x_rest, 16)
                g.partition_all_reduce(norm_all[:], norm_max[:], P, bass.bass_isa.ReduceOp.max).then_inc(ev["norm_all_done"], 1)
                reached(pool, ev["norm_all_done"], u1)
                g.tensor_tensor(norm_all[:, 2:3], norm_all[:, 2:3], norm_all[:, 3:4], ALU.add).then_inc(ev["key_min_sum_done"], 1)
                reached(pool, ev["key_min_sum_done"], u1)
                g.tensor_tensor(products[:], norm_all[:, 1:3], norm_all[:, 0:1].broadcast_to([P, 2]), ALU.mult)\
                    .then_inc(ev["products_done"], 1)
                reached(pool, ev["products_done"], u1)
                g.tensor_tensor(bounds_sq[:], products[:], signed_scale[:], ALU.mult).then_inc(ev["bounds_sq_done"], 1)
                reached_apart(pool, ev["bounds_sq_done"], u1, x_rest, 16)
                g.tensor_scalar(bounds_cut[:], bounds_sq[:], 1e-30, 1e30, ALU.max, ALU.min).then_inc(ev["bounds_cut_done"], 1)
                reached(pool, ev["bounds_cut_done"], u1)
                g.tensor_tensor(bounds[:], bounds_cut[:], half[:], ALU.pow).then_inc(ev["bounds_done"], 1)
                reached(pool, ev["bounds_done"], u1)
                g.tensor_tensor(span[:], bounds[:, 0:1], bounds[:, 1:2], ALU.add).then_inc(ev["span_done"], 1)
                g.tensor_scalar(sigma[:], bounds[:, 0:1], MAX_EXP, MAX_EXP, ALU.max, ALU.subtract).then_inc(ev["sigma_done"], 1)
                reached_apart(pool, ev["span_done"], u1, x_rest, 16)
                g.tensor_scalar(bounded_int[:, parity, :], span[:], SPAN_MAX, 1.0, ALU.is_le, ALU.mult)
                g.tensor_scalar(minus_one_if[:], span[:], SPAN_MAX, -1.0, ALU.is_le, ALU.mult).then_inc(ev["bounded_done"], 1)
                reached(pool, ev["sigma_done"], u1)
                reached(pool, ev["bounded_done"], u1)
                if probs_before is not None:
                    reached(pool, probs_ready[KT - 1][G - 1], probs_before)
                g.tensor_tensor(shift[:, parity, :], sigma[:], minus_one_if[:], ALU.mult).then_inc(ev["shift_done"], 1)

            rstd(1, moments1, var_eps1, rstd1, "moments1_done", "var1_done", "rstd1_done")
            pool.wait_ge(small_loaded, 16 * 3)
            nc.gpsimd.tensor_copy(wo_perm[:].rearrange("p q (a d) -> p q a d", d=hd),
                                  wo_in[:].rearrange("p (a q d) -> p q a d", q=2, d=hd)).then_inc(wo_permuted, 1)
            norms_of_tile(1, 0, None)
            pool.wait_ge(x_rest, 16)
            rstd(2, moments1, var_eps1, rstd1, "moments1_done", "var1_done", "rstd1_done")

            def gated_experts():
                pool.wait_ge(experts_loaded, 16)
                pool.wait_ge(setup_dve, SETUP_ALL)
                for b in range(B):
                    last = nc.gpsimd.tensor_tensor(experts_gated[:, b], experts_in[:],
                                                   spread(gates[:, b, :], 1, NE), ALU.mult)
                last.then_inc(experts_are_gated, 1)

            def gated_x(w, w1):
                b = batch_of(pool, w)
                src = x_all[:, w, :] if isinstance(w, int) else x_all[:, bass.ds(w, 1), :]
                bias = bo_gated[:, b, :] if isinstance(w, int) else bo_gated[:, bass.ds(b, 1), :]
                dst = x_gated[:] if isinstance(w, int) else x_gated[:].rearrange("p (a d) -> p a d", a=1)
                nc.gpsimd.tensor_tensor(dst, src, bias, ALU.add).then_inc(ev["x_gated_done"], 1)

            def tile(t, parity, before, after):
                w, u1, v1 = plus(pool, t, -1), plus(pool, t, 2), plus(pool, t, 3)
                if before:
                    gated_x(w, t)
                    rstd(t, moments2, var_eps2, rstd2, "moments2_done", "var2_done", "rstd2_done")
                if after:
                    norms_of_tile(u1, 1 - parity, t if before else None)
                if after == 2:
                    rstd(v1, moments1, var_eps1, rstd1, "moments1_done", "var1_done", "rstd1_done")
                if not before:
                    gated_experts()

            def last():
                gated_x(T - 1, T)
                rstd(T, moments2, var_eps2, rstd2, "moments2_done", "var2_done", "rstd2_done")
            tiles(pool, tile, last)

        @block.scalar
        def _(act):
            act.wait_ge(setup_dve, SETUP_CT)
            nc.scalar.activation(c_exp[:], cT[:], ACT.Exp, scale=-1.0).then_inc(setup_act, 1)

            def router(w1):
                reached(act, ev["logits0_done"], w1)
                nc.scalar.activation(router_exp[:], logits0[:], ACT.Exp, accum_out=router_sum[:]).then_inc(ev["router_exp_done"], 1)

            def tile(t, parity, before, after):
                t1 = plus(act, t, 1)
                reached(act, ev["shift_done"], t1)
                for k in range(KT):
                    for g in range(G):
                        reached(act, scores_ready[k][g], t1)
                        reached(act, pv_done[(k - 2) % KT], t if k < 2 else t1)
                        nc.scalar.activation(probs[:, k % 2, g, :], ps_scores[:, g, :], ACT.Exp,
                                             bias=shift[:, parity, :], scale=SCALE).then_inc(probs_ready[k][g], 1)
                    if k == 5 and before:
                        router(t)
            tiles(act, tile, lambda: router(T))

        @block.tensor
        def _(pe):
            def keep_warm(n):
                for _ in range(n):
                    nc.tensor.matmul(ps_scores[:, G - 1, HALF:HALF + P], ident_b[:], ident_b[:], start=True, stop=True)

            def modulation(chunk):
                return nc.tensor.matmul(ps_attn[:, chunk * B:(chunk + 1) * B], wmod_in[:, chunk * D:(chunk + 1) * D],
                                        siluT[:], start=True, stop=True)

            def setup_first():
                pe.wait_ge(ident_ready, 2)
                keep_warm(8)
                pe.wait_ge(c_loaded, 16)
                nc.tensor.transpose(ps_attn[:, 0:B], c_in[:], ident[0:B, 0:B]).then_inc(setup_pe, 1)
                keep_warm(10)
                pe.wait_ge(w_loaded, 16)
                for k in range(3):
                    mm = nc.tensor.transpose(ps_c[:, 0, k * P:(k + 1) * P], wqkv_in[:, k, :], ident[:])
                mm.then_inc(setup_pe, 1)
                keep_warm(7)
                pe.wait_ge(wmod_loaded, 16)
                pe.wait_ge(setup_dve, SETUP_SILU)
                modulation(0)
                modulation(1).then_inc(setup_pe, 1)

            def setup_columns():
                pe.wait_ge(setup_dve, SETUP_MOD)
                for chunk in range(2, 6):
                    modulation(chunk)
                pe.wait_ge(small_loaded, 16 * 3)
                nc.tensor.transpose(ps_attn[:, P:P + NE], router_in[:], ident[0:NE, 0:NE])
                pe.wait_ge(wo_permuted, 1)
                for odd in range(2):
                    mm = nc.tensor.transpose(ps_attn[0:R, (2 + odd) * P:(3 + odd) * P], wo_perm[:, odd, :], ident[:])
                mm.then_inc(setup_pe, 1)

            def setup_gates(k):
                for n in (2 * k, 2 * k + 1):
                    mm = nc.tensor.matmul(ps_c[:, n // B, (n % B) * D:(n % B + 1) * D],
                                          gate_cols[:, n:n + 1].broadcast_to([P, P]), ident[:], start=True, stop=True)
                mm.then_inc(setup_pe, 1)

            def a_transpose(u, u1):
                reached(pe, ev["xhat_done"], u1)
                reached(pe, chunk_saved[3], u)
                nc.tensor.transpose(ps_a[:, 0:P], xhat[:], ident[:]).then_inc(ev["xhatT_done"], 1)

            def a_project(u1):
                reached(pe, ev["hT_done"], u1)
                w = wqkvT[:].rearrange("p (j c d) -> p j c d", c=3, d=hd)
                nc.tensor.matmul(ps_a[:, 0:2 * D], hT[:], w[:, :, 0:2, :], start=True, stop=True).then_inc(ev["qk_ps_done"], 1)

            def a_project_v(u1):
                reached(pe, ev["qk_done"], u1)
                wv = wqkvT[:].rearrange("p (k o c d) -> p o k c d", o=2, c=3, d=hd)
                for g in range(G):
                    for odd in range(2):
                        mm = nc.tensor.matmul(ps_a[odd * R:(odd + 1) * R, 2 * D + g * R:2 * D + (g + 1) * R],
                                              hT[:, g * R:(g + 1) * R], wv[:, odd, :, 2, :], start=True, stop=True)
                mm.then_inc(ev["v_ps_done"], 1)

            def a_chunk(u1, ck, ps=None):
                if ck == 0:
                    reached(pe, ev["k_slots_done"], u1)
                if ck == 2:
                    reached(pe, ev["q_slots_done"], u1)
                if ps is None:
                    if ck == 0:
                        reached(pe, ev["values_done"], u1)
                    else:
                        reached(pe, chunk_saved[ck - 1], u1)
                for j in range(8):
                    mm = nc.tensor.transpose((ps_a_b if ps is None else ps)[:, j, :], slots[:, 0 if ck >= 2 else 1, 8 * (ck % 2) + j, :],
                                             ident_b[:])
                mm.then_inc(chunkT_done[ck], 1)

            def m_stage(u, parity, probs_before):
                reached_apart(pe, ev["bounded_done"], plus(pe, u, 1), setup_dve, SETUP_MOD)
                flag = pe.value_load(bounded_int[0:1, parity, :], min_val=0, max_val=1)
                with pe.If(flag == 0):
                    if probs_before is not None:
                        for g in range(G):
                            reached(pe, probs_ready[KT - 1][g], probs_before)
                    scores0, taken0 = plus(pe, u, 0) * M_PE, plus(pe, u, 0) * M_DVE
                    reached(pe, chunk_saved[3], plus(pe, u, 1))
                    for n in range(G * KT):
                        g, k = n // KT, n % KT
                        if n >= 2:
                            reached(pe, m_taken, taken0 + (n - 1))
                        for h in range(2):
                            mm = nc.tensor.matmul(ps_scores[:, n % 2, h * HALF:(h + 1) * HALF],
                                                  query_stack[:, parity, g, 2 * k:2 * k + 2, :].rearrange("p j r -> p (j r)"),
                                                  key_stack[:, parity, g, 8 * h:8 * h + 8, :].rearrange("p j r -> p (j r)"),
                                                  start=True, stop=True)
                        mm.then_inc(m_scores, 1)
                    reached(pe, m_taken, taken0 + (G * KT + 3))
                    for g in range(G):
                        rows = ps_scores[MAX_ROW:MAX_ROW + PARTS, g, 0:HALF].bitcast(BF16)
                        for k in range(KT):
                            mm = nc.tensor.transpose(rows[:, k * P:(k + 1) * P], max_parts[:, g * KT + k, :], ident_b[:],
                                                     tile_position=(0, MAX_ROW))
                        mm.then_inc(m_scores, 1)
                    reached(pe, m_taken, taken0 + M_DVE)
                with pe.Else():
                    pe.sem_inc(m_scores, M_PE)

            def scores(u1, parity, k, probs_before):
                if k == 0:
                    reached(pe, chunk_saved[3], u1)
                for g in range(G):
                    if probs_before is not None:
                        reached(pe, probs_ready[(k - 1) % KT][g], probs_before)
                    for h in range(2):
                        mm = nc.tensor.matmul(ps_scores[:, g, h * HALF:(h + 1) * HALF],
                                              key_stack[:, parity, g, 2 * k:2 * k + 2, :].rearrange("p j r -> p (j r)"),
                                              query_stack[:, parity, g, 8 * h:8 * h + 8, :].rearrange("p j r -> p (j r)"),
                                              start=True, stop=True)
                    mm.then_inc(scores_ready[k][g], 1)

            def weigh(t, t1, parity, k):
                if k == 0:
                    reached(pe, ev["attn_saved"], t)
                    reached(pe, ev["values_done"], t1)
                for g in range(G):
                    reached(pe, probs_ready[k][g], t1)
                    for h in range(2):
                        q = 32 * (2 * g + h)
                        mm = nc.tensor.matmul(ps_attn[q:q + 32, :], values[:, parity, g, k, :],
                                              probs[:, k % 2, g, h * HALF:(h + 1) * HALF],
                                              start=(k == 0), stop=(k == KT - 1), tile_position=(0, q))
                mm.then_inc(pv_done[k], 1)

            def c_attnT(w, w1):
                reached_apart(pe, ev["attn_saved"], w1, setup_dve, SETUP_ALL)
                for pair in range(4):
                    mm = nc.tensor.transpose(ps_c[:, 0, pair * P:(pair + 1) * P],
                                             attn[:, 2 * pair:2 * pair + 2, :].rearrange("p j r -> p (j r)"), ident[:])
                mm.then_inc(ev["attnT_done"], 1)

            def c_valsT(w1):
                reached_apart(pe, ev["vals_done"], w1, setup_dve, SETUP_ALL)
                for g in range(G):
                    mm = nc.tensor.transpose(ps_c[0:R, 0, g * P:(g + 1) * P], vals[:, g, :], ident[:])
                mm.then_inc(ev["valsT_ps_done"], 1)

            def c_project(w, w1):
                reached(pe, ev["valsT_done"], w1)
                b = batch_of(pe, w)
                for odd in range(2):
                    rhs = wo_gated[:, odd, b, :] if isinstance(b, int) else \
                        wo_gated[:, odd, bass.ds(b, 1), :].rearrange("p a d -> p (a d)")
                    mm = nc.tensor.matmul(ps_c[:, 1, 0:D], valsT[:, odd, :], rhs, start=(odd == 0), stop=(odd == 1))
                mm.then_inc(ev["attn_proj_done"], 1)

            def c_h2T(w1):
                reached(pe, ev["x1hat_done"], w1)
                nc.tensor.transpose(ps_c[:, 0, 0:P], x1hat[:], ident[:]).then_inc(ev["x1hatT_done"], 1)

            def c_logits(w1):
                reached(pe, ev["h2T_done"], w1)
                nc.tensor.matmul(ps_c[:, 1, 0:NE], h2T[:], routerT[:], start=True, stop=True).then_inc(ev["logits_done"], 1)

            def c_experts(w, w1, pair):
                half = pair // 2
                if pair == 0:
                    reached(pe, ev["h2T_done"], w1)
                    pe.wait_ge(experts_are_gated, 1)
                elif pair == 2:
                    reached(pe, ev["logits0_done"], w1)
                b = batch_of(pe, w)
                e0, n = pair * NE // 4, (pair % 2) * 2 * D
                if isinstance(b, int):
                    rhs = experts_gated[:, b, e0:e0 + NE // 4, :].rearrange("p e d -> p (e d)")
                else:
                    rhs = experts_gated[:, bass.ds(b, 1), e0:e0 + NE // 4, :].rearrange("p a e d -> p (a e d)")
                mm = nc.tensor.matmul(ps_c[:, half, n:n + 2 * D], h2T[:], rhs, start=True, stop=True)
                if pair % 2:
                    mm.then_inc(experts_done[half], 1)

            def tile(t, parity, before, after):
                t1, u1 = plus(pe, t, 1), plus(pe, t, 2)
                w = plus(pe, t, -1)
                for k in range(KT):
                    if k < KT - 1:
                        scores(t1, parity, k + 1, t1)
                    elif after:
                        m_stage(t1, 1 - parity, t1)
                        scores(u1, 1 - parity, 0, t1)
                    if after and k == 0:
                        a_project(u1)
                    if before and k == 2:
                        c_project(w, t)
                    if before and k == KT - 1:
                        c_experts(w, t, 2)
                        c_experts(w, t, 3)
                    if before and k == 5:
                        c_experts(w, t, 0)
                    if before and k == 6:
                        c_experts(w, t, 1)
                    weigh(t, t1, parity, k)
                    if before and k == 0:
                        c_attnT(w, t)
                    if after and k == 1:
                        a_project_v(u1)
                    if before and k == 1:
                        c_valsT(t)
                    if before and k == 4:
                        c_logits(t)
                    if after == 2 and k == 6:
                        a_transpose(u1, plus(pe, t, 3))
                    if after and 2 <= k <= 5:
                        a_chunk(u1, k - 2)
                    if before and k == 3:
                        c_h2T(t)

            def last():
                w = T - 1
                c_attnT(w, T)
                c_valsT(T)
                c_project(w, T)
                c_h2T(T)
                c_logits(T)
                for pair in range(4):
                    c_experts(w, T, pair)

            setup_first()
            a_transpose(0, 1)
            keep_warm(9)
            pe.wait_ge(setup_dve, SETUP_WQKV)
            a_project(1)
            setup_columns()
            a_project_v(1)
            keep_warm(10)
            for ck in range(4):
                a_chunk(1, ck, ps_first[ck])
            pe.wait_ge(stacks_const, 1)
            m_stage(0, 0, None)
            scores(1, 0, 0, None)
            a_transpose(1, 2)
            pe.wait_ge(setup_dve, SETUP_COLUMNS)
            for pair in range(B):
                setup_gates(pair)
            tiles(pe, tile, last)

        @block.vector
        def _(dve):
            v = nc.vector

            def step(ins):
                step.n += 1
                ins.then_inc(setup_dve, 1)
                dve.wait_ge(setup_dve, step.n)
            step.n = 0

            v.memset(slots[:].bitcast(U32)[:, :, :, SLOTS // 2:P // 2], 0)
            v.memset(values[:, :, :, :, hd + 1:32], 0.0)
            v.memset(values[:, :, :, :, hd:hd + 1], 1.0).then_inc(stacks_zero, 1)
            dve.wait_ge(stacks_zero, 1)
            v.memset(slots[:, 1, :, MAX_ROW:MAX_ROW + PARTS], 1.0).then_inc(stacks_const, 1)

            def a_moments(u, u1):
                src = x_all[:, u, :] if isinstance(u, int) else x_all[:, bass.ds(u, 1), :]
                v.bn_stats(stats1[:], src).then_inc(ev["stats1_done"], 1)
                reached_apart(dve, ev["stats1_done"], u1, x_rest, 16)
                v.bn_aggr(moments1[:], stats1[:]).then_inc(ev["moments1_done"], 1)

            def a_xhat(u, u1):
                reached(dve, ev["rstd1_done"], u1)
                reached(dve, ev["moments1_done"], u1)
                src = x_all[:, u, :] if isinstance(u, int) else x_all[:, bass.ds(u, 1), :]
                dst = xhat[:] if isinstance(u, int) else xhat[:].rearrange("p (a d) -> p a d", a=1)
                v.tensor_scalar(dst, src, moments1[:, 0:1], rstd1[:], ALU.subtract, ALU.mult).then_inc(ev["xhat_done"], 1)

            def mod_col(u, k):
                return mod_tab[:, u, k:k + 1] if isinstance(u, int) else \
                    mod_tab[:, bass.ds(u, 1), k:k + 1].rearrange("p a k -> p (a k)")

            def a_hT(u, u1):
                reached(dve, ev["xhatT_done"], u1)
                v.tensor_scalar(hT[:], ps_a[:, 0:P], mod_col(u, 1), mod_col(u, 0), ALU.mult, ALU.add).then_inc(ev["hT_done"], 1)

            def a_qk(u1):
                reached(dve, ev["qk_ps_done"], u1)
                bias = bqkv_rows[:].rearrange("p (j c d) -> p c j d", c=3, d=hd)
                v.tensor_tensor(qk[:], ps_a[:, 0:2 * D].rearrange("p (j c d) -> p c j d", j=J, c=2), bias[:, 0:2],
                                ALU.add).then_inc(ev["qk_done"], 1)

            def a_split(u1):
                part = [parts[:, :, :, a, :].rearrange("p c j d -> p (c j) d") for a in range(PARTS)]
                q = qk[:].rearrange("p c j d -> p (c j) d")
                rest = qk_rest[:].rearrange("p c j d -> p (c j) d")
                reached(dve, ev["qk_done"], u1)
                v.tensor_copy(part[0], q).then_inc(ev["hi_done"], 1)
                reached(dve, ev["hi_done"], u1)
                v.tensor_tensor(rest, q, part[0], ALU.subtract).then_inc(ev["rest1_done"], 1)
                reached(dve, ev["rest1_done"], u1)
                v.tensor_copy(part[1], rest).then_inc(ev["mid_done"], 1)
                reached(dve, ev["mid_done"], u1)
                v.tensor_tensor(part[2], rest, part[1], ALU.subtract).then_inc(ev["parts_done"], 1)

            def a_values(u1, parity):
                reached(dve, ev["v_ps_done"], u1)
                v.tensor_tensor(values[:, parity, :, :, 0:hd],
                                ps_a[:, 2 * D:2 * D + G * R].rearrange("p (g k d) -> p g k d", g=G, d=hd),
                                spread(bv[:], 1, G),
                                ALU.add).then_inc(ev["values_done"], 1)

            def a_slots(u1):
                reached(dve, ev["parts_done"], u1)
                v.tensor_copy(slots[:, 1, :, 0:SLOTS].rearrange("p j (a m) -> p j a m", a=PARTS),
                              spread(parts[:, 1].rearrange("p j b d -> p j (b d)"), 2, PARTS)).then_inc(ev["k_slots_done"], 1)
                v.tensor_copy(slots[:, 0, :, 0:SLOTS].rearrange("p j (a b d) -> p j a b d", a=PARTS, b=PARTS),
                              spread(parts[:, 0], 3, PARTS)).then_inc(ev["q_slots_done"], 1)

            def a_norms(u1):
                flat = squares[:].rearrange("p c j d -> p (c j d)")
                src = qk[:].rearrange("p c j d -> p (c j d)")
                reached(dve, ev["qk_done"], u1)
                v.tensor_tensor(flat, src, src, ALU.mult).then_inc(ev["squares_done"], 1)
                reached(dve, ev["squares_done"], u1)
                v.tensor_reduce(norms[:], squares[:].rearrange("p c j d -> p (c j) d"), AX.X, ALU.add)\
                    .then_inc(ev["norms_done"], 1)
                reached(dve, ev["norms_done"], u1)
                v.tensor_reduce(key_min[:], norms[:, J:2 * J], AX.X, ALU.min).then_inc(ev["key_min_done"], 1)
                v.tensor_reduce(norm_max[:, 0:2], norms[:].rearrange("p (c j) -> p c j", c=2), AX.X, ALU.max)
                reached(dve, ev["key_min_done"], u1)
                v.tensor_scalar(norm_max[:, 2:2 + G], head_far[:], key_min[:], None, ALU.subtract)\
                    .then_inc(ev["norm_max_done"], 1)

            def a_save_chunk(u1, parity, ck, scores_before, ps=None):
                reached(dve, chunkT_done[ck], u1)
                if ck == 0 and scores_before is not None:
                    reached(dve, scores_ready[KT - 1][G - 1], scores_before)
                v.tensor_copy(shape_chunk(ck, parity), (ps_a_b if ps is None else ps).rearrange("p j (g r) -> p j g r", g=G))\
                    .then_inc(chunk_saved[ck], 1)

            def load_bounded(u1, parity):
                reached_apart(dve, ev["bounded_done"], u1, x_rest, 16)
                return dve.value_load(bounded_int[0:1, parity, :], min_val=0, max_val=1)

            def m_stage(u, parity, is_bounded):
                with dve.If(is_bounded == 0):
                    scores0, taken0 = plus(dve, u, 0) * M_PE, plus(dve, u, 0) * M_DVE
                    for n in range(G * KT):
                        reached(dve, m_scores, scores0 + (n + 1))
                        v.tensor_reduce(row_max[:, n:n + 1], ps_scores[:, n % 2, :], AX.X, ALU.max).then_inc(m_taken, 1)
                    reached(dve, m_taken, taken0 + G * KT)
                    v.tensor_scalar(max_parts[:, :, 0], row_max[:], -1.0, None, ALU.mult)
                    v.tensor_scalar(max_rest[:], row_max[:], -1.0, None, ALU.mult).then_inc(m_taken, 1)
                    reached(dve, m_taken, taken0 + (G * KT + 1))
                    v.tensor_tensor(max_rest2[:], max_rest[:], max_parts[:, :, 0], ALU.subtract)
                    v.tensor_tensor(max_parts[:, :, 1], max_rest[:], max_parts[:, :, 0], ALU.subtract).then_inc(m_taken, 1)
                    reached(dve, m_taken, taken0 + (G * KT + 2))
                    v.tensor_tensor(max_parts[:, :, 2], max_rest2[:], max_parts[:, :, 1], ALU.subtract).then_inc(m_taken, 1)
                    for g in range(G):
                        reached(dve, m_scores, scores0 + (G * KT + 1 + g))
                        v.tensor_copy(query_stack[MAX_ROW:MAX_ROW + PARTS, parity, g].rearrange("p j r -> p (j r)"),
                                      ps_scores[MAX_ROW:MAX_ROW + PARTS, g, 0:HALF].bitcast(BF16)).then_inc(m_taken, 1)
                with dve.Else():
                    dve.sem_inc(m_taken, M_DVE)

            def c_save(w1):
                reached(dve, pv_done[KT - 1], w1)
                v.tensor_copy(attn[:].rearrange("p j r -> p (j r)"), ps_attn[:]).then_inc(ev["attn_saved"], 1)

            def c_vals(w, w1):
                reached(dve, ev["attnT_done"], w1)
                ps = ps_c[:, 0, :].rearrange("p (j c m) -> p j c m", j=4, c=4)
                v.reciprocal(sums_inv[:], ps[:, :, :, hd]).then_inc(ev["sums_inv_done"], 1)
                reached(dve, ev["sums_inv_done"], w1)
                v.tensor_tensor(vals[:].rearrange("p g (h j d) -> p j (g h) d", h=2, d=hd), ps[:, :, :, 0:hd],
                                spread(sums_inv[:], 3, hd), ALU.mult).then_inc(ev["vals_done"], 1)

            def c_valsT(w1):
                reached(dve, ev["valsT_ps_done"], w1)
                v.tensor_copy(valsT[:].rearrange("p o (g r) -> p g o r", g=G),
                              ps_c[0:R, 0, 0:G * P].rearrange("p (g o r) -> p g o r", g=G, o=2)).then_inc(ev["valsT_done"], 1)

            def c_x1(w1):
                reached(dve, ev["attn_proj_done"], w1)
                reached(dve, ev["x_gated_done"], w1)
                v.tensor_tensor(x1[:], ps_c[:, 1, 0:D], x_gated[:], ALU.add).then_inc(ev["x1_done"], 1)
                reached(dve, ev["x1_done"], w1)
                v.bn_stats(stats2[:], x1[:]).then_inc(ev["stats2_done"], 1)
                reached_apart(dve, ev["stats2_done"], w1, x_rest, 16)
                v.bn_aggr(moments2[:], stats2[:]).then_inc(ev["moments2_done"], 1)

            def c_x1hat(w1):
                reached(dve, ev["rstd2_done"], w1)
                reached(dve, ev["moments2_done"], w1)
                v.tensor_scalar(x1hat[:], x1[:], moments2[:, 0:1], rstd2[:], ALU.subtract, ALU.mult)\
                    .then_inc(ev["x1hat_done"], 1)

            def c_h2T(w, w1):
                reached(dve, ev["x1hatT_done"], w1)
                v.tensor_scalar(h2T[:], ps_c[:, 0, 0:P], mod_col(w, 3), mod_col(w, 2), ALU.mult, ALU.add)\
                    .then_inc(ev["h2T_done"], 1)

            def c_logits(w1):
                reached_apart(dve, ev["logits_done"], w1, x_rest, 16)
                v.max(top_logits[:], ps_c[:, 1, 0:NE]).then_inc(ev["top_logits_done"], 1)
                reached(dve, ev["top_logits_done"], w1)
                v.tensor_scalar(logits0[:], ps_c[:, 1, 0:NE], top_logits[:, 0:1], None, ALU.subtract)\
                    .then_inc(ev["logits0_done"], 1)

            def c_router_top(w1):
                reached(dve, ev["router_exp_done"], w1)
                v.reciprocal(router_inv[:], router_sum[:]).then_inc(ev["router_inv_done"], 1)
                reached(dve, ev["router_inv_done"], w1)
                v.tensor_scalar(router_p[:], router_exp[:], router_inv[:], None, ALU.mult).then_inc(ev["router_p_done"], 1)
                reached_apart(dve, ev["router_p_done"], w1, x_rest, 16)
                v.max(top_p[:], router_p[:]).then_inc(ev["top_p_done"], 1)
                reached_apart(dve, ev["top_p_done"], w1, x_rest, 16)
                v.max_index(top_id[:], top_p[:], router_p[:]).then_inc(ev["top_id_done"], 1)
                v.tensor_tensor(pair_sum[:], top_p[:, 0:1], top_p[:, 1:2], ALU.add).then_inc(ev["pair_sum_done"], 1)
                reached(dve, ev["top_id_done"], w1)
                v.tensor_copy(top_idf[:], top_id[:]).then_inc(ev["top_idf_done"], 1)
                reached(dve, ev["pair_sum_done"], w1)
                v.tensor_scalar(pair_eps[:], pair_sum[:], TOP_EPS, None, ALU.add).then_inc(ev["pair_eps_done"], 1)

            def c_router_weights(w1):
                reached(dve, ev["pair_eps_done"], w1)
                v.reciprocal(pair_inv[:], pair_eps[:]).then_inc(ev["pair_inv_done"], 1)
                reached(dve, ev["pair_inv_done"], w1)
                v.tensor_scalar(pair_w[:], top_p[:, 0:2], pair_inv[:], None, ALU.mult).then_inc(ev["pair_w_done"], 1)
                reached(dve, ev["pair_w_done"], w1)
                reached(dve, ev["top_idf_done"], w1)
                v.tensor_scalar(coef0[:], expert_ids[:], top_idf[:, 0:1], pair_w[:, 0:1], ALU.is_equal, ALU.mult)\
                    .then_inc(ev["coef0_done"], 1)
                v.tensor_scalar(coef1[:], expert_ids[:], top_idf[:, 1:2], pair_w[:, 1:2], ALU.is_equal, ALU.mult)\
                    .then_inc(ev["coef1_done"], 1)
                v.tensor_tensor(pair_pw[:], top_p[:, 0:2], pair_w[:], ALU.mult).then_inc(ev["pair_pw_done"], 1)
                reached(dve, ev["pair_pw_done"], w1)
                v.tensor_tensor(bias_w[:], pair_pw[:, 0:1], pair_pw[:, 1:2], ALU.add).then_inc(ev["bias_w_done"], 1)
                reached(dve, ev["coef0_done"], w1)
                reached(dve, ev["coef1_done"], w1)
                v.tensor_tensor(coef[:], coef0[:], coef1[:], ALU.add).then_inc(ev["coef_done"], 1)

            def c_weigh(w, w1):
                b = batch_of(dve, w)
                reached(dve, ev["bias_w_done"], w1)
                gate = gates[:, b, :] if isinstance(b, int) else gates[:, bass.ds(b, 1), :].rearrange("p a d -> p (a d)")
                v.scalar_tensor_tensor(out=base[:], in0=gate, scalar=bias_w[:], in1=x1[:], op0=ALU.mult,
                                       op1=ALU.add).then_inc(ev["base_done"], 1)
                reached(dve, experts_done[1], w1)
                reached(dve, ev["coef_done"], w1)
                v.tensor_tensor(weighted[:], ps_c[:].rearrange("p h (e d) -> p (h e) d", d=D),
                                spread(coef[:], 2, D), ALU.mult)\
                    .then_inc(ev["weighted_done"], 1)

            def c_mix(w, w1):
                reached(dve, ev["weighted_done"], w1)
                v.tensor_reduce(mixed[:], weighted[:].rearrange("p e d -> p d e"), AX.X, ALU.add)\
                    .then_inc(ev["mixed_done"], 1)
                reached(dve, ev["mixed_done"], w1)
                reached(dve, ev["base_done"], w1)
                if isinstance(w, int):
                    v.tensor_tensor(out_all[:, w, :], base[:], mixed[:], ALU.add).then_inc(ev["out_done"], 1)
                else:
                    v.tensor_tensor(out_all[:, bass.ds(w, 1), :], base[:].rearrange("p (a d) -> p a d", a=1),
                                    mixed[:].rearrange("p (a d) -> p a d", a=1), ALU.add).then_inc(ev["out_done"], 1)

            def gated_weights():
                dve.wait_ge(setup_pe, 4 + B)
                gate1 = ps_c[:, 0, :].rearrange("p (b d) -> p b d", b=B)
                for odd in range(2):
                    v.tensor_tensor(wo_gated[:, odd], spread(woT[:, odd, :], 1, B), gate1[0:R], ALU.mult)
                v.tensor_tensor(bo_gated[:], spread(bo_rows[:], 1, B), gate1, ALU.mult)
                step(v.tensor_copy(gates[:].rearrange("p b d -> p (b d)"), ps_c[:, 1, :]))
                assert step.n == SETUP_ALL

            def tile(t, parity, before, after):
                u, u1, w = plus(dve, t, 1), plus(dve, t, 2), plus(dve, t, -1)
                nn, nn1 = plus(dve, t, 2), plus(dve, t, 3)
                other = 1 - parity
                if before:
                    c_save(t)
                if before == 2:
                    c_mix(plus(dve, t, -2), w)
                if before:
                    c_vals(w, t)
                if after:
                    a_qk(u1)
                    a_split(u1)
                if before:
                    c_valsT(t)
                if after:
                    a_slots(u1)
                    a_values(u1, other)
                if not before:
                    gated_weights()
                if before:
                    c_x1(t)
                if after:
                    a_save_chunk(u1, other, 0, t)
                if before:
                    c_x1hat(t)
                if after:
                    a_norms(u1)
                if before:
                    c_h2T(w, t)
                if after:
                    a_save_chunk(u1, other, 1, None)
                if before:
                    c_logits(t)
                if after == 2:
                    a_moments(nn, nn1)
                if after:
                    a_save_chunk(u1, other, 2, None)
                if before:
                    c_router_top(t)
                if after == 2:
                    a_xhat(nn, nn1)
                if after:
                    a_save_chunk(u1, other, 3, None)
                if before:
                    c_router_weights(t)
                if after == 2:
                    a_hT(nn, nn1)
                if after:
                    is_bounded = load_bounded(u1, other)
                    m_stage(u, other, is_bounded)
                if before:
                    c_weigh(w, t)

            def last():
                w = T - 1
                c_save(T)
                c_vals(w, T)
                c_valsT(T)
                c_mix(T - 2, T - 1)
                c_x1(T)
                c_x1hat(T)
                c_h2T(w, T)
                c_logits(T)
                c_router_top(T)
                c_router_weights(T)
                c_weigh(w, T)
                c_mix(w, T)

            def save_modulation(k, chunk):
                dst = mod_tab[:].rearrange("p (b i) k -> p b i k", i=TB)[:, :, :, k]
                src = spread(ps_attn[:, chunk * B:(chunk + 1) * B], 2, TB)
                return v.tensor_scalar(dst, src, float(k % 2), None, ALU.add)

            dve.wait_ge(x_first, 16)
            a_moments(0, 1)
            dve.wait_ge(setup_pe, 1)
            step(v.tensor_copy(cT[:], ps_attn[:, 0:B]))
            assert step.n == SETUP_CT
            dve.wait_ge(setup_act, 1)
            step(v.tensor_scalar(c_exp1[:], c_exp[:], 1.0, None, ALU.add))
            step(v.reciprocal(c_sig[:], c_exp1[:]))
            step(v.tensor_tensor(siluT[:], cT[:], c_sig[:], ALU.mult))
            assert step.n == SETUP_SILU
            a_xhat(0, 1)
            dve.wait_ge(setup_pe, 2)
            step(v.tensor_copy(wqkvT[:], ps_c[:, 0, 0:3 * D]))
            assert step.n == SETUP_WQKV
            dve.wait_ge(setup_pe, 3)
            save_modulation(0, 0)
            step(save_modulation(1, 1))
            assert step.n == SETUP_MOD
            a_hT(0, 1)
            dve.wait_ge(bqkv_loaded, 16)
            bq = bqkv_rows[:].rearrange("p (k o c d) -> p o k c d", o=2, c=3, d=hd)
            for odd in range(2):
                ins = v.tensor_copy(bv[odd * R:(odd + 1) * R], bq[odd * R:(odd + 1) * R, odd, :, 2, :])
            ins.then_inc(bv_ready, 1)
            a_qk(1)
            dve.wait_ge(pool_consts, 1 + G)
            a_norms(1)
            a_split(1)
            a_slots(1)
            dve.wait_ge(bv_ready, 1)
            a_values(1, 0)
            for ck in range(4):
                a_save_chunk(1, 0, ck, None, ps_first[ck])
            m_stage(0, 0, load_bounded(1, 0))
            dve.wait_ge(x_rest, 16)
            a_moments(1, 2)
            dve.wait_ge(setup_pe, 4)
            save_modulation(2, 3)
            save_modulation(3, 4)
            v.tensor_copy(routerT[:], ps_attn[:, P:P + NE])
            v.tensor_copy(woT[:].rearrange("p o d -> p (o d)"), ps_attn[0:R, 2 * P:4 * P])
            gate_ps = ps_attn[:, 0:6 * B].rearrange("p (k c b) -> p k c b", k=2, c=3)[:, :, 2, :]
            step(v.tensor_scalar(gate_flag[:].rearrange("p (k b) -> p k b", k=2), gate_ps, 0.0, 2.0, ALU.is_ge, ALU.mult))
            step(v.tensor_scalar(gate_sign[:], gate_flag[:], -1.0, None, ALU.add))
            step(v.tensor_tensor(gate_size[:].rearrange("p (k b) -> p k b", k=2), gate_ps,
                                 gate_sign[:].rearrange("p (k b) -> p k b", k=2), ALU.mult))
            step(v.scalar_tensor_tensor(out=gate_cols[:], in0=gate_size[:], scalar=GATE_MIN, in1=gate_sign[:],
                                        op0=ALU.max, op1=ALU.mult))
            assert step.n == SETUP_COLUMNS
            a_xhat(1, 2)
            a_hT(1, 2)
            tiles(dve, tile, last)


_INS = ["L0_attn_x", "L0_attn_Wqkv", "L0_attn_bqkv", "L0_attn_Wo", "L0_attn_bo", "L0_ffn_router_w",
        "L0_ffn_expert_weights", "L0_c", "L0_wmod"]
_OUTS = [((4, 1024, 128), "float32")]


def kernel(**inputs):
    import numpy as _np
    import concourse.bacc as _bacc
    from concourse import mybir as _mybir
    from concourse.bass_utils import run_bass_kernel_spmd as _run

    nc = _bacc.Bacc("TRN2", target_bir_lowering=False, num_devices=1)
    arrays, args = {}, []
    for name in _INS:
        a = _np.ascontiguousarray(inputs[name])
        arrays[f"in_{name}_dram"] = a
        args.append(nc.dram_tensor(f"in_{name}_dram", a.shape, _mybir.dt.from_np(a.dtype), kind="ExternalInput").ap())
    for i, (shape, dtype) in enumerate(_OUTS):
        dt = _mybir.dt.from_np(_np.dtype(dtype))
        args.append(nc.dram_tensor(f"out_{i}_dram", shape, dt, kind="ExternalOutput").ap())
    adaln_block(nc, *args)
    r = _run(nc, [arrays], core_ids=[0])
    got = tuple(r.results[0][f"out_{i}_dram"] for i in range(len(_OUTS)))
    return got[0]
```
